# Optimizing a Trainium2 kernel written in Bass

```python
import numpy as np
import jax
import jax.numpy as jnp

def _softmax(x, axis=-1):
    return jax.nn.softmax(x, axis=axis)

def _gelu(x):
    return jax.nn.gelu(x, approximate=True)

def _silu(x):
    return jax.nn.silu(x)

def _sigmoid(x):
    return jax.nn.sigmoid(x)

def _layernorm(x, axis=-1, eps=1e-05):
    m = jnp.mean(x, axis=axis, keepdims=True)
    v = jnp.var(x, axis=axis, keepdims=True)
    return (x - m) / jnp.sqrt(v + eps)

def _scatter_add(tgt, idx, src, axis=0):
    return tgt.at[idx].add(src)

def _segment_sum(src, seg, n):
    return jax.ops.segment_sum(src, seg, n)
kernel_name = 'mk_recurrent_d1_jaxref_r4_19575c'

def setup_inputs(seed: int=0):
    np.random.seed(seed)
    _w = jnp.asarray

    def _L0_attn_setup():
        import jax, jax.numpy as jnp
        import numpy as np

        def soft_clamp(x, lo, hi, sharpness):
            c = (hi + lo) / 2.0
            r = (hi - lo) / 2.0
            xn = (x - c) / (r + 1e-08)
            return jnp.tanh(xn * sharpness) / sharpness * r + c
        key = jax.random.key(seed)
        ks = jax.random.split(key, 7)
        B, L, D, N = (2, 512, 256, 16)
        x = jax.random.normal(ks[0], (B, L, D), dtype=jnp.float32)
        Wdt = jax.random.normal(ks[1], (D, D), dtype=jnp.float32) * 0.02
        bdt = jnp.full((D,), -2.0, dtype=jnp.float32)
        WB = jax.random.normal(ks[2], (N, D), dtype=jnp.float32) * (1.0 / np.sqrt(D))
        WC = jax.random.normal(ks[3], (N, D), dtype=jnp.float32) * (1.0 / np.sqrt(D))
        A_log = jax.random.normal(ks[4], (D, N), dtype=jnp.float32) * 0.1
        Dp = jnp.full((D,), 0.1, dtype=jnp.float32)
        return {'x': x, 'Wdt': Wdt, 'bdt': bdt, 'WB': WB, 'WC': WC, 'A_log': A_log, 'Dp': Dp}
    _L0_attn_in = _L0_attn_setup()

    def _L0_ffn_setup():
        import jax, jax.numpy as jnp
        import numpy as np
        import math
        N_EXP = 8
        TOP_K = 2
        CAPACITY_FACTOR = 1.25

        def _capacity(num_tokens):
            cap = math.floor(TOP_K * CAPACITY_FACTOR * num_tokens / N_EXP)
            cap += cap % 2
            return int(cap)
        key = jax.random.key(seed)
        k1, k2, k3, k4 = jax.random.split(key, 4)
        B, C, d = (4, 256, 256)
        x = jax.random.normal(k1, (B, C, d), dtype=jnp.float32)
        w_g = jax.random.normal(k2, (d, N_EXP), dtype=jnp.float32) * 0.02
        c_fc = jax.random.normal(k3, (N_EXP, d, 4 * d), dtype=jnp.float32) * 0.02
        c_proj = jax.random.normal(k4, (N_EXP, 4 * d, d), dtype=jnp.float32) * 0.02
        return {'x': x, 'w_g': w_g, 'c_fc': c_fc, 'c_proj': c_proj}
    _L0_ffn_in = _L0_ffn_setup()
    _d = {'L0_attn_x': _L0_attn_in['x'], 'L0_attn_Wdt': _L0_attn_in['Wdt'], 'L0_attn_bdt': _L0_attn_in['bdt'], 'L0_attn_WB': _L0_attn_in['WB'], 'L0_attn_WC': _L0_attn_in['WC'], 'L0_attn_A_log': _L0_attn_in['A_log'], 'L0_attn_Dp': _L0_attn_in['Dp'], 'L0_ffn_w_g': _L0_ffn_in['w_g'], 'L0_ffn_c_fc': _L0_ffn_in['c_fc'], 'L0_ffn_c_proj': _L0_ffn_in['c_proj']}
    _x0 = _d['L0_attn_x']
    _d['L0_attn_x'] = jax.random.normal(jax.random.fold_in(jax.random.key(seed), 1), (4, 1024, 256), dtype=_x0.dtype)
    del _x0
    return _d

def reference(L0_attn_x, L0_attn_Wdt, L0_attn_bdt, L0_attn_WB, L0_attn_WC, L0_attn_A_log, L0_attn_Dp, L0_ffn_w_g, L0_ffn_c_fc, L0_ffn_c_proj):

    def _L0_attn_ref(x, Wdt, bdt, WB, WC, A_log, Dp):
        import jax, jax.numpy as jnp
        import numpy as np

        def soft_clamp(x, lo, hi, sharpness):
            c = (hi + lo) / 2.0
            r = (hi - lo) / 2.0
            xn = (x - c) / (r + 1e-08)
            return jnp.tanh(xn * sharpness) / sharpness * r + c
        dt = soft_clamp(jax.nn.softplus(x @ Wdt.T + bdt), 0.001, 0.1, 0.5)
        B_param = x @ WB.T
        C_param = x @ WC.T
        A = -jnp.exp(soft_clamp(A_log, -5.0, 5.0, 0.5))
        dt_A = soft_clamp(dt[..., None] * A[None, None], -8.0, 8.0, 0.5)
        dA = jnp.exp(dt_A)
        dB = dt[..., None] * B_param[:, :, None, :]
        dA_t = jnp.moveaxis(dA, 1, 0)
        dB_t = jnp.moveaxis(dB, 1, 0)
        x_t = jnp.moveaxis(x, 1, 0)
        C_t = jnp.moveaxis(C_param, 1, 0)
        h0 = jnp.zeros(x.shape[:1] + (x.shape[2], A.shape[1]), dtype=jnp.float32)

        def step(h, inp):
            dAt, dBt, xt, Ct = inp
            h = dAt * h + dBt * xt[..., None]
            h_norm = jnp.sqrt(jnp.sum(h * h, axis=(1, 2), keepdims=True))
            scale = jnp.minimum(20.0 / (h_norm + 1e-08), 1.0)
            h = h * scale
            y = jnp.einsum('bdn,bn->bd', h, Ct) + Dp * xt
            return (h, y)
        _, ys = jax.lax.scan(step, h0, (dA_t, dB_t, x_t, C_t))
        return jnp.moveaxis(ys, 0, 1)

    def _L0_ffn_ref(x, w_g, c_fc, c_proj):
        import jax, jax.numpy as jnp
        import numpy as np
        import math
        N_EXP = 8
        TOP_K = 2
        CAPACITY_FACTOR = 1.25

        def _capacity(num_tokens):
            cap = math.floor(TOP_K * CAPACITY_FACTOR * num_tokens / N_EXP)
            cap += cap % 2
            return int(cap)
        B, C, d = x.shape
        T = B * C
        cap = _capacity(T)
        xt = x.reshape(T, d)
        logits = xt @ w_g
        top_v, top_i = jax.lax.top_k(logits, TOP_K)
        full = jnp.full_like(logits, -jnp.inf)
        full = full.at[jnp.arange(T)[:, None], top_i].set(top_v)
        probs = jax.nn.softmax(full, axis=-1)
        exp_mask = jax.nn.one_hot(top_i, N_EXP, dtype=jnp.int32)
        exp_mask = jnp.transpose(exp_mask, (1, 0, 2))
        exp_rank = jnp.cumsum(exp_mask.reshape(TOP_K * T, N_EXP), axis=0) - 1
        exp_rank = exp_rank.reshape(TOP_K, T, N_EXP)
        exp_mask = exp_mask * (exp_rank < cap).astype(jnp.int32)
        exp_rank = jnp.sum(exp_mask * exp_rank, axis=-1)
        exp_weights = exp_mask.astype(x.dtype) * probs[None]
        rank_oh = jax.nn.one_hot(exp_rank, cap, dtype=x.dtype)
        cb_weight = jnp.einsum('kte,ktc->tec', exp_weights, rank_oh)
        sec_mask = (cb_weight != 0).astype(x.dtype)
        exp_batches = jnp.einsum('tec,td->ecd', sec_mask, xt)
        h = jax.nn.gelu(jnp.einsum('ecd,edf->ecf', exp_batches, c_fc), approximate=False)
        exp_out = jnp.einsum('ecf,efd->ecd', h, c_proj)
        out = cb_weight.reshape(T, N_EXP * cap) @ exp_out.reshape(N_EXP * cap, d)
        return out.reshape(B, C, d)
    x = L0_attn_x
    xn = _layernorm(x, axis=-1)
    s = _L0_attn_ref(xn, L0_attn_Wdt, L0_attn_bdt, L0_attn_WB, L0_attn_WC, L0_attn_A_log, L0_attn_Dp)
    g = _silu(_L0_ffn_ref(xn, L0_ffn_w_g, L0_ffn_c_fc, L0_ffn_c_proj))
    x = x + s * g
    return x

_drawn_inputs = setup_inputs


def setup_inputs(seed=0):
    import zlib

    import numpy as np

    out = dict(_drawn_inputs(seed))
    spreads = {'L0_attn_bdt': (-2.0, 0.6), 'L0_attn_Dp': (0.10000000149011612, 0.6)}
    factors = {'L0_attn_Wdt': 8.0, 'L0_attn_A_log': 8.0}
    for name, (base, spread) in spreads.items():
        noise = np.random.default_rng([zlib.crc32(name.encode()), seed]).standard_normal(out[name].shape)
        drawn = base * np.exp(spread * noise) if base else spread * noise
        out[name] = jnp.asarray(drawn.astype(out[name].dtype))
    for name, factor in factors.items():
        out[name] = (out[name] * factor).astype(out[name].dtype)
    return out
```

```python
from contextlib import ExitStack

import concourse.bass as bass
from concourse import mybir

NB, NT, D, NS = 4, 1024, 256, 16
NE, CAP, FF = 8, 1280, 1024
P = 128
DH = D // P
TOK = NB * NT
TILES = TOK // P
CH = NT // P
HALF = 64
NHALF = NT // HALF
BLK = 16
NBLK = NT // BLK
BPB = P // BLK
QUAD = 4
RING = 2 * BLK
SLOTS = NE * CAP
TS = 256
TPE = CAP // TS
PADROWS = 2 * TS
TRASH = SLOTS + PADROWS
XE_ROWS = TRASH + 2 * TOK
YPAD = 2 * BLK
FC = FF // P
CLAMP = 20.0
DT_LO, DT_HI, SHARP = 0.001, 0.1, 0.5
DT_C, DT_R = (DT_HI + DT_LO) / 2, (DT_HI - DT_LO) / 2
WIN = 2 * BLK - 1
NG = NB * DH
CONSTS = 22


def build(nc, x, wdtT, bdt, wb, wc, a_log, dpar, w_g, c_fc, c_proj, out):
    f32, bf16, i32 = mybir.dt.float32, mybir.dt.bfloat16, mybir.dt.int32
    ALU, ACT, AX = mybir.AluOpType, mybir.ActivationFunctionType, mybir.AxisListType
    ctx = ExitStack()
    with ctx:
        def sb(name, shape, dt=f32):
            return ctx.enter_context(nc.sbuf_tensor(name, shape, dt))

        def sem(name):
            return ctx.enter_context(nc.semaphore(name))

        xe = nc.dram_tensor("xe", (XE_ROWS, D), f32, kind="Internal").ap()
        ye = nc.dram_tensor("ye", (SLOTS, D), f32, kind="Internal").ap()
        feed = nc.dram_tensor("feed", (NHALF + 1, P, 2, NB * DH * HALF), f32, kind="Internal").ap()
        dx = nc.dram_tensor("dx", (NT + YPAD, NB, D), f32, kind="Internal").ap()
        ys = nc.dram_tensor("ys", (NT + YPAD, NB, D), f32, kind="Internal").ap()

        ident = sb("ident", [P, P])
        ones = sb("ones", [P, P])
        bsum = sb("bsum", [P, P])
        winmask = sb("winmask", [P, 8])
        zeros = sb("zeros", [P, 2 * D])
        exps = sb("exps", [P, 2])
        neghalf = sb("neghalf", [P, NB])
        pick = sb("pick", [P, BLK, P])
        dtbias = sb("dtbias", [P, 1])
        a16 = sb("a16", [P, DH * NS])
        be = sb("be", [P, NT, 2])
        ccol = sb("ccol", [P, BLK + NT])
        mv = sb("mv", [P, TILES, 2])
        rstd = sb("rstd", [P, TILES])
        wsel = sb("wsel", [P, 2, TILES])
        src_i = sb("src_i", [P, 2, TILES], i32)
        dst_i = sb("dst_i", [P, 2, TILES], i32)

        ARENA = 40704
        arena = sb("arena", [P, ARENA])
        at = [0]

        def take(n):
            at[0] += n
            assert at[0] <= ARENA, at[0]
            return arena[:, at[0] - n:at[0]]

        SD = NB * DH * HALF
        tanhb = take(2 * P * HALF).rearrange("p (f s t) -> p f s t", f=2, t=HALF)
        stage = take(2 * 2 * SD).rearrange("p (f w s) -> p f w s", f=2, w=2)
        da = take(RING * P).rearrange("p (t d) -> p t d", d=P)
        ur = take(RING * P).rearrange("p (t d) -> p t d", d=P)
        hr = take(RING * P).rearrange("p (t d) -> p t d", d=P)
        win = take(BLK * NG * WIN).rearrange("p (t c g) -> p t c g", g=NG, c=WIN)
        xt = take(DH * TS).rearrange("p (k s) -> p k s", k=DH)
        hid = take(FC * TS).rearrange("p (k s) -> p k s", k=FC)
        xrow = take(2 * D).rearrange("p (c d) -> p c d", c=2)
        yrow = take(2 * D).rearrange("p (c d) -> p c d", c=2)
        wf = sb("wf", [P, DH, FF])
        wp = sb("wp", [P, FC, D])
        yx = take(2 * P).rearrange("p (w d) -> p w d", w=2)
        dxt = take(P)
        vv = take(P)
        junk = take(2 * P).rearrange("p (f d) -> p f d", f=2)
        junkq = take(64)
        ac = take(2)
        tr = take(64)
        qv = take(1)
        mx = take(1)
        sv = take(RING * 2).rearrange("p (t w) -> p t w", w=2)
        cs = take(BLK)
        ring_be = take(RING * 2).rearrange("p (t w) -> p t w", w=2)

        at2 = [0]

        def lay(n):
            at2[0] += n
            assert at2[0] <= ARENA, at2[0]
            return arena[:, at2[0] - n:at2[0]]

        xnat = lay(TILES * D).rearrange("p (b i d) -> p b i d", b=NB, i=CH)
        xnT = lay(CH * DH * NB * P).rearrange("p (i k b t) -> p i k b t", i=CH, k=DH, b=NB)
        spl = lay(CH * DH * NB * P).rearrange("p (i k m) -> p i k m", i=CH, k=DH)
        rel = lay(2 * DH * NB * P).rearrange("p (f k m) -> p f k m", f=2, k=DH)
        fst = lay(2 * 2 * 2 * SD).rearrange("p (f h w s) -> p f h w s", f=2, h=2, w=2)
        sq = lay(DH * NB * P).rearrange("p (k m) -> p k m", k=DH)
        sqb = lay(P)
        dsb = lay(P)
        dxn = lay(2 * NB * D).rearrange("p (f b d) -> p f b d", f=2, b=NB)
        wdt_sb = lay(DH * D).rearrange("p (k m) -> p k m", k=DH)
        wb_sb = lay(DH * 32).rearrange("p (k m) -> p k m", k=DH)
        wc_sb = lay(DH * 32).rearrange("p (k m) -> p k m", k=DH)
        wg_sb = lay(DH * NE).rearrange("p (k m) -> p k m", k=DH)
        dpb = lay(D)
        bdt_sb = lay(DH)
        stats = lay(2 * NB * 6).rearrange("p (f b s) -> p f b s", f=2, b=NB)
        vare = lay(CH * NB).rearrange("p (i b) -> p i b", i=CH)
        JT = TILES
        lg = lay(NE * JT).rearrange("p (e j) -> p e j", e=NE)
        lgw = lay(NE * JT).rearrange("p (e j) -> p e j", e=NE)
        iom = lay(NE * JT).rearrange("p (e j) -> p e j", e=NE)
        iom_i = lay(NE * JT).bitcast(i32).rearrange("p (e j) -> p e j", e=NE)
        tmp = lay(NE * JT).rearrange("p (e j) -> p e j", e=NE)
        ohb = lay(NE * 2 * JT).rearrange("p (e k j) -> p e k j", e=NE, k=2)
        ohf = lay(NE * 2 * JT).rearrange("p (e k j) -> p e k j", e=NE, k=2)
        rkt = lay(NE * 2 * JT).rearrange("p (e k j) -> p e k j", e=NE, k=2)
        tot = lay(NE * 2 * JT).rearrange("p (e k j) -> p e k j", e=NE, k=2)
        inc = lay(NE * 2 * JT).rearrange("p (e k j) -> p e k j", e=NE, k=2)
        keepm = lay(NE * 2 * JT).rearrange("p (e k j) -> p e k j", e=NE, k=2)
        lows = lay(P)
        top = lay(2 * JT).rearrange("p (k j) -> p k j", k=2)
        eix = lay(2 * JT).rearrange("p (k j) -> p k j", k=2)
        rank = lay(2 * JT).rearrange("p (k j) -> p k j", k=2)
        keep = lay(2 * JT).rearrange("p (k j) -> p k j", k=2)
        row = lay(2 * JT).rearrange("p (k j) -> p k j", k=2)
        trash = lay(2 * JT).rearrange("p (k j) -> p k j", k=2)
        trash_i = lay(2 * JT).bitcast(i32).rearrange("p (k j) -> p k j", k=2)
        pw = lay(4 * JT).rearrange("p (k j) -> p k j", k=4)
        alog = lay(DH * NS)
        prologue_words = at2[0]

        at3 = [0]

        def end(n):
            at3[0] += n
            assert at3[0] <= ARENA, at3[0]
            return arena[:, at3[0] - n:at3[0]]

        GR = 4
        xl = end(2 * GR * D).rearrange("p (f g d) -> p f g d", f=2, g=GR)
        yl = end(2 * GR * D).rearrange("p (f g d) -> p f g d", f=2, g=GR)
        g0 = end(2 * GR * D).rearrange("p (f g d) -> p f g d", f=2, g=GR)
        g1 = end(2 * GR * D).rearrange("p (f g d) -> p f g d", f=2, g=GR)
        fm = end(2 * GR * D).rearrange("p (f g d) -> p f g d", f=2, g=GR)
        sl = end(2 * GR * D).rearrange("p (f g d) -> p f g d", f=2, g=GR)
        ol = end(2 * GR * D).rearrange("p (f g d) -> p f g d", f=2, g=GR)

        ps = [ctx.enter_context(nc.psum_tensor(f"ps{i}", [P, 512], f32)) for i in range(8)]

        ld_x = [sem(f"ld_x{k}") for k in range(CH)]
        ld_w = sem("ld_w")
        ld_v = sem("ld_v")
        memz = sem("memz")
        padz = sem("padz")
        consts = sem("consts")
        stat_chain = sem("stat_chain")
        stat_ready = sem("stat_ready")
        rstd_ready = sem("rstd_ready")
        xn_ready = sem("xn_ready")
        xt_ps = sem("xt_ps")
        xt_sb = sem("xt_sb")
        z_ps = sem("z_ps")
        z_used = sem("z_used")
        act_chain = sem("act_chain")
        sp_half = sem("sp_half")
        sp_ready = sem("sp_ready")
        th_ready = sem("th_ready")
        bc_ps = sem("bc_ps")
        bc_sb = sem("bc_sb")
        sq_ready = sem("sq_ready")
        sqb_ready = sem("sqb_ready")
        e_ps = sem("e_ps")
        e_chain = sem("e_chain")
        e_used = sem("e_used")
        dt_ready = sem("dt_ready")
        fst_ready = sem("fst_ready")
        fst_done = [sem(f"fst_done{k}") for k in range(2)]
        dxn_ready = sem("dxn_ready")
        dx_done = [sem(f"dx_done{k}") for k in range(2)]
        lg_ps = sem("lg_ps")
        rt_in = sem("rt_in")
        rank_ps = sem("rank_ps")
        rt_chain = sem("rt_chain")
        gap_ready = sem("gap_ready")
        gap_exp = sem("gap_exp")
        route_ready = sem("route_ready")
        a_tanh = sem("a_tanh")
        a_exp = sem("a_exp")
        a_ready = sem("a_ready")
        scat_done = sem("scat_done")
        loop_go = sem("loop_go")
        init_win = sem("init_win")
        T_ready = sem("T_ready")
        h_ready = sem("h_ready")
        q_ready = sem("q_ready")
        v_ready = sem("v_ready")
        m_ready = sem("m_ready")
        s_ready = sem("s_ready")
        ac_ready = sem("ac_ready")
        ta_ps = sem("ta_ps")
        exp_done = sem("exp_done")
        tu_ps = sem("tu_ps")
        u_done = sem("u_done")
        be_stage = sem("be_stage")
        tanh_done = sem("tanh_done")
        stage_in = sem("stage_in")
        cs_ready = sem("cs_ready")
        win_ready = sem("win_ready")
        y_done = sem("y_done")
        y_sb = sem("y_sb")
        x0_ps = sem("x0_ps")
        y_out = sem("y_out")
        dx_in = sem("dx_in")
        xrow_in = sem("xrow_in")
        xt_tp = sem("xt_tp")
        xt_in = sem("xt_in")
        mm1_ps = sem("mm1_ps")
        gelu_done = sem("gelu_done")
        mm2_ps = sem("mm2_ps")
        ye_sb = sem("ye_sb")
        ye_out = sem("ye_out")
        wf_in = sem("wf_in")
        wp_in = sem("wp_in")
        fin_x = [sem(f"fin_x{k}") for k in range(2)]
        fin_y = [sem(f"fin_y{k}") for k in range(2)]
        fin_g = [sem(f"fin_g{k}") for k in range(2)]
        f_half = sem("f_half")
        f_ready = sem("f_ready")
        silu_done = sem("silu_done")
        f_mul = sem("f_mul")
        o_ready = sem("o_ready")
        o_out = [sem(f"o_out{k}") for k in range(2)]

        xn_tok = x.rearrange("b (i p) d -> p b i d", p=P)
        dx_tok = dx[YPAD:].rearrange("(i p) b d -> p i b d", p=P)
        ys_tok = ys[YPAD:].rearrange("(i p) b d -> p i b d", p=P)
        out_tok = out.rearrange("b (i p) d -> p b i d", p=P)

        work = []
        for i in range(TPE):
            work += [("up", i, j, 4) for j in range(FC // 2)] + [("turn", i, 0, 4)] + [("down", i, c, 8) for c in range(2)]
        total = sum(w[3] for w in work)
        by_block, n = [[] for _ in range(BPB)], 0
        for w in work:
            by_block[min(BPB - 1, n * BPB // total)].append(w)
            n += w[3]

        block = ctx.enter_context(nc.Block())

        @block.sync
        def _(sp):
            for i in range(CH):
                sp.dma_start(xnat[:, :, i, :], xn_tok[:, :, i, :]).then_inc(ld_x[i], 16)
            sp.dma_start(wdt_sb, wdtT.rearrange("(k p) m -> p k m", p=P)).then_inc(ld_w, 16)
            sp.dma_start(wb_sb, wb.rearrange("(k p) m -> p k m", p=P)).then_inc(ld_w, 16)
            sp.dma_start(wc_sb, wc.rearrange("(k p) m -> p k m", p=P)).then_inc(ld_w, 16)
            sp.dma_start(wg_sb, w_g.rearrange("(k p) m -> p k m", p=P)).then_inc(ld_w, 16)
            sp.dma_start(bdt_sb, bdt.rearrange("(k p) -> p k", p=P), allow_slow_non_contiguous=True).then_inc(ld_v, 16)
            sp.dma_start(alog.rearrange("p (k n) -> p k n", k=DH), a_log.rearrange("(k p) n -> p k n", p=P)).then_inc(ld_v, 16)
            sp.dma_start(dpb, dpar.rearrange("(a d) -> a d", a=1).broadcast_to([P, D])).then_inc(ld_v, 16)
            sp.wait_ge(memz, 1)
            sp.dma_start(xe[0:TRASH, :].rearrange("(r p) d -> p r d", p=P),
                         zeros[:, 0:D].unsqueeze(1).broadcast_to([P, TRASH // P, D])).then_inc(padz, 16)
            for b in range(NB):
                sp.dma_start(dx[0:YPAD, b, :], zeros[0:YPAD, 0:D]).then_inc(padz, 16)
            for i in range(CH):
                sp.wait_ge(dxn_ready, i + 1)
                sp.dma_start(dx_tok[:, i], dxn[:, i % 2]).then_inc(dx_done[i % 2], 16)
            for i in range(CH):
                sp.wait_ge(fst_ready, i + 1)
                for h in range(2):
                    sp.dma_start(feed[2 * i + h], fst[:, i % 2, h, :, :]).then_inc(fst_done[i % 2], 16)
            sp.dma_start(feed[NHALF], fst[:, 1, 1, :, :]).then_inc(fst_done[0], 16)
            sp.wait_ge(fst_done[0], 16 * (CH + 1))
            sp.wait_ge(fst_done[1], 16 * CH)
            for k in range(2):
                sp.wait_ge(dx_done[k], 16 * CH // 2)
            sp.sem_inc(loop_go, 1)
            sp.wait_ge(loop_go, 5)
            sp.sem_inc(y_out, 1)
            sp.sem_inc(ye_out, 1)
            sp.dma_start(stage[:, 0, :, :], feed[0]).then_inc(stage_in, 16)
            sp.dma_start(xrow, xe[0:TS, :].rearrange("(c p) d -> p c d", p=P)).then_inc(xrow_in, 16)
            sp.wait_ge(xt_tp, 1)
            sp.dma_start(xrow, xe[TS:2 * TS, :].rearrange("(c p) d -> p c d", p=P)).then_inc(xrow_in, 16)

            def load_dx(n, at):
                sp.wait_ge(y_done, n + 1)
                sp.dma_start(dxt, dx[at, :, :].rearrange("t b (k d) -> (t b k) d", k=DH)).then_inc(dx_in, 16)

            def store_y(n, at):
                sp.wait_ge(y_sb, n + 2)
                sp.dma_start(ys[at, :, :].rearrange("t b (k d) -> (t b k) d", k=DH), yx[:, 0, :]).then_inc(y_out, 16)

            with sp.Fori(0, CH) as m:
                sp.wait_ge(mm1_ps, m * (TPE * FC // 2) + 1)
                sp.dma_start(wf[:, :, :], c_fc[bass.ds(m, 1), :, :].rearrange("e (k p) f -> p (e k) f", p=P)).then_inc(wf_in, 16)
                sp.wait_ge(mm2_ps, m * (TPE * 2) + 1)
                sp.dma_start(wp[:, :, :], c_proj[bass.ds(m, 1), :, :].rearrange("e (k p) d -> p (e k) d", p=P)).then_inc(wp_in, 16)
                for g in range(BPB):
                    if g % 4 == 0:
                        f = g // 4
                        sp.wait_ge(tanh_done, m * 2 + f + 1)
                        sp.dma_start(stage[:, 1 - f, :, :].rearrange("p w s -> p (w s)"),
                                     feed[bass.ds(m * 2 + f + 1, 1), :, :, :].rearrange("h p w s -> p (h w s)")).then_inc(stage_in, 16)
                    load_dx(m * BPB + g, bass.ds(m * P + g * BLK, BLK))
                    for kind, i, j, _ in by_block[g]:
                        if kind == "turn":
                            sp.wait_ge(xt_tp, m * TPE + i + 2)
                            sp.dma_start(xrow, xe[bass.ds(m * CAP + (i + 2) * TS, TS), :]
                                         .rearrange("(c p) d -> p c d", p=P)).then_inc(xrow_in, 16)
                        if kind == "down" and j == 1:
                            sp.wait_ge(ye_sb, m * TPE + i + 2)
                            sp.dma_start(ye[bass.ds(m * CAP + i * TS, TS), :]
                                         .rearrange("(c p) d -> p c d", p=P), yrow).then_inc(ye_out, 16)
                    store_y(m * BPB + g, bass.ds(m * P + g * BLK, BLK))
            for n in range(NBLK, NBLK + 2):
                load_dx(n, slice(n * BLK, (n + 1) * BLK))
                store_y(n, slice(n * BLK, (n + 1) * BLK))
            sp.wait_ge(tanh_done, NHALF + 1)
            sp.wait_ge(ta_ps, NT // QUAD + 1)
            sp.wait_ge(y_out, 16 * (NBLK + 2) + 1)
            for i in range(CH):
                if i >= 2:
                    sp.wait_ge(o_ready, i - 1)
                sp.dma_start(xl[:, i % 2], xn_tok[:, :, i, :]).then_inc(fin_x[i % 2], 16)
                sp.dma_start(yl[:, i % 2], ys_tok[:, i]).then_inc(fin_y[i % 2], 16)
                if i >= 1:
                    sp.wait_ge(o_ready, i)
                    sp.dma_start(out_tok[:, :, i - 1, :], ol[:, (i - 1) % 2]).then_inc(o_out[(i - 1) % 2], 16)
            sp.wait_ge(o_ready, CH)
            sp.dma_start(out_tok[:, :, CH - 1, :], ol[:, (CH - 1) % 2]).then_inc(o_out[(CH - 1) % 2], 16)
            for k in range(2):
                sp.wait_ge(o_out[k], 16 * CH // 2)
            sp.wait_ge(padz, 16 * (NB + 1))
            sp.wait_ge(ye_out, 16 * NE * TPE + 1)

        @block.gpsimd
        def _(pool):
            g = nc.gpsimd
            n = [0]

            def made(ins):
                n[0] += 1
                ins.then_inc(consts, 1)

            g.memset(zeros[:, :], 0.0).then_inc(memz, 1)
            made(g.memset(ident[:, :], 0.0))
            made(g.memset(ones[:, :], 1.0))
            made(g.memset(pick[:, :, :], 0.0))
            made(g.memset(bsum[:, :], 0.5))
            made(g.memset(winmask[:, :], 1.0))
            made(g.memset(exps[:, 0:1], -1.0))
            made(g.memset(exps[:, 1:2], -0.5))
            made(g.memset(neghalf[:, :], -0.5))
            made(g.memset(dtbias[:, :], -DT_C * SHARP / (DT_R + 1e-8)))
            made(g.memset(lows, 1.0))
            made(g.memset(keepm, 1.0))
            made(g.memset(ccol[:, 0:BLK], 0.0))
            made(g.iota(iom_i, pattern=[[1, NE], [0, JT]], base=-NE, channel_multiplier=0))
            made(g.iota(trash_i, pattern=[[TOK, 2], [P, JT]], base=TRASH, channel_multiplier=1))
            pool.wait_ge(consts, n[0])
            made(g.affine_select(out=ident[:, :], in_=ident[:, :], compare_op=ALU.not_equal, fill=1.0, base=0,
                                 pattern=[[-1, P]], channel_multiplier=1))
            pk = pick[:, :, :].rearrange("p t (g n) -> p t g n", g=NG)
            made(g.affine_select(out=pk, in_=pk, compare_op=ALU.not_equal, fill=1.0, base=0,
                                 pattern=[[-NG, BLK], [-1, NG], [0, NS]], channel_multiplier=1))
            q4 = bsum[:, :].rearrange("p (b c) -> p b c", b=NB)
            made(g.affine_select(out=q4, in_=q4, compare_op=ALU.is_ge, fill=0.0, base=0,
                                 pattern=[[-32, NB], [0, 32]], channel_multiplier=1))
            made(g.affine_select(out=winmask[:, :], in_=winmask[:, :], compare_op=ALU.is_ge, fill=0.0, base=0,
                                 pattern=[[-NS, NG]], channel_multiplier=1))
            made(g.affine_select(out=lows, in_=lows, compare_op=ALU.is_gt, fill=0.0, base=0,
                                 pattern=[[1, P]], channel_multiplier=-1))
            made(g.memset(keepm[:, :, 0, 0:1], 0.0))
            pool.wait_ge(consts, n[0])
            made(g.affine_select(out=q4, in_=q4, compare_op=ALU.is_ge, fill=0.0, base=31,
                                 pattern=[[32, NB], [0, 32]], channel_multiplier=-1))
            made(g.affine_select(out=winmask[:, :], in_=winmask[:, :], compare_op=ALU.is_ge, fill=0.0, base=NS - 1,
                                 pattern=[[NS, NG]], channel_multiplier=-1))
            assert n[0] == CONSTS, n[0]
            rs = rstd[:, :].rearrange("p (b i) -> p b i", b=NB)
            for i in range(CH):
                pool.wait_ge(stat_ready, i + 1)
                g.tensor_tensor(rs[:, :, i], vare[:, i, :], neghalf[:, :], ALU.pow).then_inc(rstd_ready, 1)
            pool.wait_ge(padz, 16 * (NB + 1))
            pool.wait_ge(route_ready, 1)
            pool.wait_ge(xn_ready, CH)
            for b in range(NB):
                for i in range(CH):
                    for k in range(2):
                        g.indirect_dma_start(
                            out=xe, out_offset=bass.IndirectOffsetOnAxis(ap=dst_i[:, k, b * CH + i:b * CH + i + 1], axis=0),
                            in_=xnat[:, b, i, :], in_offset=None,
                            bounds_check=XE_ROWS - 1, oob_is_err=True).then_inc(scat_done, 16)
            pool.wait_ge(scat_done, 16 * 2 * TILES)
            pool.sem_inc(loop_go, 1)
            pool.wait_ge(loop_go, 5)
            g.memset(win, 0.0).then_inc(init_win, 1)
            g.memset(sv, 1.0).then_inc(init_win, 1)
            pool.wait_ge(init_win, 2)
            pool.sem_inc(win_ready, 1)
            pool.sem_inc(s_ready, BLK)

            def scale_of(slot, count):
                pool.wait_ge(m_ready, count)
                g.tensor_tensor(sv[:, slot, :], mx.broadcast_to([P, 2]), exps[:, :], ALU.pow).then_inc(s_ready, 1)

            def windows(half, ccols, count, blk):
                pool.wait_ge(s_ready, count)
                g.tensor_tensor(cs, ccols, sv[:, half * BLK:(half + 1) * BLK, 1], ALU.mult).then_inc(cs_ready, 1)
                pool.wait_ge(cs_ready, blk)
                pool.wait_ge(y_done, blk + 1)
                g.tensor_tensor(win[:, :, BLK - 1, :], cs.unsqueeze(2).broadcast_to([P, BLK, NG]),
                                winmask[:, :].unsqueeze(1).broadcast_to([P, BLK, NG]), ALU.mult).then_inc(win_ready, 1)

            with pool.Fori(0, NT // RING) as r:
                for k in range(RING):
                    scale_of((k - 1) % RING, r * RING + (k + 1 + BLK))
                    if k % BLK == 0:
                        windows(1 - k // BLK, ccol[:, bass.ds(r * RING + k, BLK)], r * RING + (k + 1 + BLK), r * 2 + (k // BLK + 1))
            scale_of(RING - 1, NT + 1 + BLK)
            windows(1, ccol[:, NT:NT + BLK], NT + 1 + BLK, NBLK + 1)
            pool.wait_ge(ye_out, 16 * NE * TPE + 1)
            pool.wait_ge(tanh_done, NHALF + 1)
            pool.wait_ge(ta_ps, NT // QUAD + 1)
            for i in range(CH):
                if i >= 2:
                    pool.wait_ge(f_ready, NB * (i - 1))
                for b in range(NB):
                    for k, to in enumerate((g0, g1)):
                        g.indirect_dma_start(
                            out=to[:, i % 2, b, :], out_offset=None, in_=ye,
                            in_offset=bass.IndirectOffsetOnAxis(ap=src_i[:, k, b * CH + i:b * CH + i + 1], axis=0),
                            bounds_check=SLOTS - 1, oob_is_err=True).then_inc(fin_g[i % 2], 16)

        @block.vector
        def _(dve):
            v = nc.vector

            links = [0]

            def link(ins):
                links[0] += 1
                ins.then_inc(stat_chain, 1)
                dve.wait_ge(stat_chain, links[0])

            mvt = mv[:, :, :].rearrange("p (b i) s -> p b i s", b=NB)

            def statistics(i):
                dve.wait_ge(ld_x[i], 16)
                for b in range(NB):
                    last = v.bn_stats(out=stats[:, i % 2, b, :], in_=xnat[:, b, i, :])
                link(last)
                for b in range(NB):
                    last = v.bn_aggr(out=mvt[:, b, i, :], in_=stats[:, i % 2, b, :])
                link(last)
                v.tensor_scalar(vare[:, i, :], mvt[:, :, i, 1], 1e-5, None, ALU.add).then_inc(stat_ready, 1)

            def normalize(i):
                dve.wait_ge(rstd_ready, i + 1)
                for b in range(NB):
                    j = b * CH + i
                    last = v.tensor_scalar(xnat[:, b, i, :], xnat[:, b, i, :], mv[:, j, 0:1], rstd[:, j:j + 1],
                                           ALU.subtract, ALU.mult)
                last.then_inc(xn_ready, 1)
                dve.wait_ge(xn_ready, i + 1)
                if i >= 2:
                    dve.wait_ge(dx_done[i % 2], 16 * (i // 2))
                v.tensor_tensor(dxn[:, i % 2, :, :], xnat[:, :, i, :], dpb.unsqueeze(1).broadcast_to([P, NB, D]),
                                ALU.mult).then_inc(dxn_ready, 1)

            dve.wait_ge(ld_v, 48)
            statistics(0)
            for i in range(CH):
                if i + 1 < CH:
                    statistics(i + 1)
                normalize(i)
            dve.wait_ge(consts, CONSTS)
            dve.wait_ge(a_exp, 1)
            v.tensor_scalar(a16[:, :], alog, -1.0 / 16.0, None, ALU.mult).then_inc(a_ready, 1)
            for i in range(CH):
                dve.wait_ge(sp_half, i + 1)
                v.tensor_tensor(spl[:, i], spl[:, i], rel[:, i % 2], ALU.add).then_inc(sp_ready, 1)
                dve.wait_ge(bc_ps, i + 1)
                v.tensor_copy(be[:, i * P:(i + 1) * P, 0], ps[4][:, 0:P])
                v.tensor_copy(ccol[:, BLK + i * P:BLK + (i + 1) * P], ps[4][:, P:2 * P]).then_inc(bc_sb, 1)

            hops = [0]

            def hop(ins):
                hops[0] += 1
                ins.then_inc(rt_chain, 1)
                dve.wait_ge(rt_chain, hops[0])

            dve.wait_ge(lg_ps, 1)
            hop(v.tensor_copy(iom, iom_i))
            hop(v.tensor_copy(trash, trash_i))
            hop(v.tensor_copy(lg, ps[6][:, 0:NE * JT].rearrange("p (j e) -> p e j", e=NE)))
            for k in range(2):
                cur = lg if k == 0 else lgw
                hop(v.tensor_reduce(out=top[:, k, :], in_=cur.rearrange("p e j -> p j e"), axis=AX.X, op=ALU.max))
                hop(v.tensor_tensor(tmp, cur, top[:, k, :].unsqueeze(1).broadcast_to([P, NE, JT]), ALU.is_equal))
                hop(v.tensor_tensor(tmp, tmp, iom, ALU.mult))
                hop(v.tensor_reduce(out=eix[:, k, :], in_=tmp.rearrange("p e j -> p j e"), axis=AX.X, op=ALU.min))
                hop(v.tensor_tensor(ohf[:, :, k, :], iom, eix[:, k, :].unsqueeze(1).broadcast_to([P, NE, JT]), ALU.is_equal))
                if k == 0:
                    hop(v.scalar_tensor_tensor(lgw, ohf[:, :, 0, :], -3e38, lg, ALU.mult, ALU.add))
            v.tensor_tensor(pw[:, 0, :], top[:, 1, :], top[:, 0, :], ALU.subtract).then_inc(gap_ready, 1)
            v.tensor_copy(ohb, ohf).then_inc(rt_in, 1)
            dve.wait_ge(gap_exp, 1)
            hop(v.tensor_scalar(pw[:, 1, :], pw[:, 3, :], 1.0, None, ALU.add))
            hop(v.reciprocal(pw[:, 2, :], pw[:, 1, :]))
            hop(v.tensor_tensor(pw[:, 3, :], pw[:, 3, :], pw[:, 2, :], ALU.mult))
            dve.wait_ge(rank_ps, 1)
            kj = "p e k j -> p (e k j)"
            hop(v.tensor_copy(tot, ps[6][:, :].rearrange("p (e k j) -> p e k j", e=NE, k=2)))
            hop(v.tensor_tensor_scan(inc.rearrange(kj), keepm.rearrange(kj), tot.rearrange(kj), 0.0, ALU.mult, ALU.add))
            hop(v.tensor_tensor(inc, inc, tot, ALU.subtract))
            hop(v.tensor_tensor(inc, inc, ps[7][:, :].rearrange("p (e k j) -> p e k j", e=NE, k=2), ALU.add))
            hop(v.tensor_tensor(inc, inc, ohf, ALU.mult))
            hop(v.tensor_reduce(out=rank, in_=inc.rearrange("p e k j -> p k j e"), axis=AX.X, op=ALU.add))
            hop(v.tensor_scalar(keep, rank, float(CAP), None, ALU.is_lt))
            hop(v.tensor_scalar(row, eix, float(NE), float(CAP), ALU.add, ALU.mult))
            hop(v.tensor_tensor(row, row, rank, ALU.add))
            hop(v.tensor_tensor(rank, row, keep, ALU.mult))
            hop(v.tensor_copy(src_i[:, :, :], rank))
            hop(v.tensor_tensor(row, row, trash, ALU.subtract))
            hop(v.tensor_tensor(row, row, keep, ALU.mult))
            hop(v.tensor_tensor(row, row, trash, ALU.add))
            v.tensor_copy(dst_i[:, :, :], row)
            v.tensor_tensor(wsel[:, :, :], pw[:, 2:4, :], keep, ALU.mult).then_inc(route_ready, 1)

            for i in range(CH):
                dve.wait_ge(th_ready, i + 1)
                if i >= 2:
                    dve.wait_ge(fst_done[i % 2], 32 * (i // 2))
                for h in range(2):
                    to = fst[:, i % 2, h, 0, :].rearrange("p (b k t) -> p k b t", b=NB, k=DH)
                    tv = spl[:, i].rearrange("p k (b h t) -> p h k b t", b=NB, h=2)[:, h]
                    for k in range(DH):
                        last = v.tensor_scalar(to[:, k], tv[:, k], DT_R / SHARP, DT_C, ALU.mult, ALU.add)
                last.then_inc(dt_ready, 1)
                dve.wait_ge(dt_ready, i + 1)
                if i >= 1:
                    dve.wait_ge(sq_ready, i)
                for h in range(2):
                    dtv = fst[:, i % 2, h, 0, :].rearrange("p (b k t) -> p k b t", b=NB, k=DH)
                    to = fst[:, i % 2, h, 1, :].rearrange("p (t b k) -> p k b t", b=NB, k=DH)
                    xv = xnT[:, i].rearrange("p k b (h t) -> p h k b t", h=2)[:, h]
                    for k in range(DH):
                        last = v.tensor_tensor(to[:, k], dtv[:, k], xv[:, k], ALU.mult)
                last.then_inc(fst_ready, 1)
                v.tensor_tensor(sqb, be[:, i * P:(i + 1) * P, 0], be[:, i * P:(i + 1) * P, 0], ALU.mult).then_inc(sqb_ready, 1)
                dve.wait_ge(e_ps, i + 1)
                v.tensor_copy(dsb, ps[5][:, P:2 * P]).then_inc(e_chain, 1)
                dve.wait_ge(e_chain, i + 1)
                v.scalar_tensor_tensor(be[:, i * P:(i + 1) * P, 1], ps[5][:, 0:P], 1.0 / CLAMP ** 2, dsb,
                                       ALU.mult, ALU.mult).then_inc(e_used, 1)
            dve.wait_ge(e_used, CH)
            dve.wait_ge(route_ready, 1)
            dve.sem_inc(loop_go, 1)
            dve.wait_ge(loop_go, 5)

            for s_, c_ in ((T_ready, BLK), (v_ready, BLK), (ac_ready, BLK), (m_ready, BLK), (h_ready, BLK), (q_ready, BLK)):
                dve.sem_inc(s_, c_)
            v.memset(hr, 0.0).then_inc(h_ready, 1)
            v.memset(qv, 1.0).then_inc(q_ready, 1)
            svb = lambda slot: sv[:, slot, :].unsqueeze(2).broadcast_to([P, 2, 32])
            tr2 = tr.rearrange("p (w c) -> p w c", w=2)
            with dve.Fori(0, NT // RING) as r:
                for k in range(RING):
                    before = (k - 1) % RING
                    now = r * RING + (k + 1 + BLK)
                    dve.wait_ge(h_ready, now)
                    if k % QUAD == 0:
                        dve.wait_ge(exp_done, r * (RING // QUAD) + (k // QUAD + 3))
                    v.tensor_tensor(vv, hr[:, before, :], da[:, k, :], ALU.mult).then_inc(v_ready, 1)
                    dve.wait_ge(q_ready, now)
                    v.tensor_scalar(mx, qv, 1.0, None, ALU.max).then_inc(m_ready, 1)
                    dve.wait_ge(v_ready, now)
                    if k % QUAD == 0:
                        dve.wait_ge(u_done, r * (RING // QUAD) + (k // QUAD + 2))
                    v.tensor_tensor_reduce(out=junk[:, 0, :], in0=vv, in1=ur[:, k, :], scale=2.0, scalar=0.0,
                                           op0=ALU.mult, op1=ALU.add, accum_out=ac[:, 1:2])
                    v.tensor_tensor_reduce(out=junk[:, 1, :], in0=vv, in1=vv, scale=1.0, scalar=0.0,
                                           op0=ALU.mult, op1=ALU.add, accum_out=ac[:, 0:1]).then_inc(ac_ready, 1)
                    dve.wait_ge(ac_ready, now)
                    v.transpose(tr, ac.unsqueeze(2).broadcast_to([P, 2, 32])).then_inc(T_ready, 1)
                    dve.wait_ge(s_ready, now)
                    if k % BLK == 0:
                        dve.wait_ge(y_done, r * 2 + (k // BLK + 2))
                        dve.wait_ge(be_stage, r * 2 + (k // BLK + 1))
                    v.scalar_tensor_tensor(hr[:, k, :], vv, sv[:, before, 1:2], ur[:, k, :], ALU.mult, ALU.add)\
                        .then_inc(h_ready, 1)
                    dve.wait_ge(T_ready, now)
                    v.tensor_tensor_reduce(out=junkq.rearrange("p (w c) -> p w c", w=2), in0=tr2, in1=svb(before),
                                           scale=1.0 / CLAMP ** 2, scalar=ring_be[:, k, 1:2],
                                           op0=ALU.mult, op1=ALU.add, accum_out=qv).then_inc(q_ready, 1)
            dve.wait_ge(q_ready, NT + 1 + BLK)
            v.tensor_scalar(mx, qv, 1.0, None, ALU.max).then_inc(m_ready, 1)

            def last_product(i):
                f = i % 2
                dve.wait_ge(silu_done, i + 1)
                dve.wait_ge(fin_x[f], 16 * (i // 2 + 1))
                dve.wait_ge(fin_y[f], 16 * (i // 2 + 1))
                v.tensor_tensor(sl[:, f], sl[:, f], yl[:, f], ALU.mult).then_inc(f_mul, 1)
                dve.wait_ge(f_mul, i + 1)
                if i >= 2:
                    dve.wait_ge(o_out[f], 16 * (i // 2))
                v.tensor_tensor(ol[:, f], sl[:, f], xl[:, f], ALU.add).then_inc(o_ready, 1)

            for i in range(CH):
                f = i % 2
                dve.wait_ge(fin_g[f], 16 * 2 * NB * (i // 2 + 1))
                if i >= 2:
                    dve.wait_ge(silu_done, i - 1)
                for b in range(NB):
                    v.tensor_scalar(fm[:, f, b, :], g0[:, f, b, :], wsel[:, 0, b * CH + i:b * CH + i + 1], None,
                                    ALU.mult).then_inc(f_half, 1)
                for b in range(NB):
                    dve.wait_ge(f_half, NB * i + b + 1)
                    v.scalar_tensor_tensor(fm[:, f, b, :], g1[:, f, b, :], wsel[:, 1, b * CH + i:b * CH + i + 1],
                                           fm[:, f, b, :], ALU.mult, ALU.add).then_inc(f_ready, 1)
                if i >= 1:
                    last_product(i - 1)
            last_product(CH - 1)


        @block.scalar
        def _(act):
            a = nc.scalar
            links = [0]

            def link(ins):
                links[0] += 1
                ins.then_inc(act_chain, 1)
                act.wait_ge(act_chain, links[0])

            act.wait_ge(ld_v, 48)
            act.wait_ge(consts, CONSTS)
            a.activation(alog, alog, ACT.Tanh, scale=0.1).then_inc(a_tanh, 1)
            act.wait_ge(a_tanh, 1)
            a.activation(alog, alog, ACT.Exp, scale=10.0).then_inc(a_exp, 1)
            a.preload_act_table_set("natural_log_exp_and_others")
            for i in range(CH):
                act.wait_ge(xt_ps, i + 1)
                for k in range(DH):
                    last = a.activation(xnT[:, i, k].rearrange("p b t -> p (b t)"), ps[k][:, :], ACT.Copy)
                last.then_inc(xt_sb, 1)
                act.wait_ge(z_ps, i + 1)
                if i >= 2:
                    act.wait_ge(sp_ready, i - 1)
                for k in range(DH):
                    a.activation(rel[:, i % 2, k, :], ps[2 + k][:, :], ACT.Relu, bias=bdt_sb[:, k:k + 1])
                    last = a.activation(spl[:, i, k, :], ps[2 + k][:, :], ACT.Abs, bias=bdt_sb[:, k:k + 1])
                last.then_inc(z_used, 1)
                act.wait_ge(z_used, i + 1)
                link(a.activation(spl[:, i], spl[:, i], ACT.Exp, scale=-1.0))
                a.activation(spl[:, i], spl[:, i], ACT.Ln, bias=1.0).then_inc(sp_half, 1)
            act.wait_ge(gap_ready, 1)
            a.activation(pw[:, 3, :], pw[:, 0, :], ACT.Exp).then_inc(gap_exp, 1)
            for i in range(CH):
                act.wait_ge(sp_ready, i + 1)
                a.activation(spl[:, i], spl[:, i], ACT.Tanh, bias=dtbias[:, :], scale=SHARP / (DT_R + 1e-8)).then_inc(th_ready, 1)
            for i in range(CH):
                act.wait_ge(fst_ready, i + 1)
                if i >= 1:
                    act.wait_ge(e_ps, i)
                for h in range(2):
                    for b in range(NB):
                        last = a.activation(sq.rearrange("p k (b h t) -> p h b k t", b=NB, h=2)[:, h, b],
                                            fst[:, i % 2, h, 1, :].rearrange("p (t b k) -> p b k t", b=NB, k=DH)[:, b],
                                            ACT.Square)
                last.then_inc(sq_ready, 1)
            act.wait_ge(sq_ready, CH)
            act.sem_inc(loop_go, 1)
            act.wait_ge(loop_go, 5)
            act.sem_inc(exp_done, 2)
            act.sem_inc(u_done, 1)
            act.sem_inc(gelu_done, 2)
            act.sem_inc(ye_sb, 1)

            def tanh_ops(f, first, count):
                src = stage[:, f, 0, :].rearrange("p (b k t) -> p b k t", b=NB, k=DH)
                dst = tanhb[:, f, :, :].rearrange("p (b k n) t -> p b k n t", b=NB, k=DH)
                for c in range(first, first + count):
                    k, n_ = divmod(c, NS)
                    last = a.activation(dst[:, :, k, n_, :], src[:, :, k, :], ACT.Tanh, scale=a16[:, c:c + 1])
                return last

            act.wait_ge(a_ready, 1)
            act.wait_ge(stage_in, 16)
            tanh_ops(0, 0, DH * NS).then_inc(tanh_done, 1)
            act.wait_ge(x0_ps, 1)
            a.activation(yx[:, 1, :], ps[3][:, P:2 * P], ACT.Copy).then_inc(y_sb, 1)
            act.wait_ge(xt_tp, 1)
            a.activation(xt.rearrange("p k s -> p (k s)"), ps[6][:, :], ACT.Copy).then_inc(xt_in, 1)

            def y_out_of_psum(n):
                act.wait_ge(y_done, n + 2)
                act.wait_ge(y_out, n * 16 + 1)
                a.activation(yx.rearrange("p w d -> p (w d)"), ps[3][:, 0:2 * P], ACT.Copy).then_inc(y_sb, 1)

            with act.Fori(0, CH) as m:
                for g in range(BPB):
                    half = g % 2
                    act.wait_ge(q_ready, m * P + (g * BLK + 1))
                    a.activation(ring_be[:, half * BLK:(half + 1) * BLK, :], be[:, bass.ds(m * P + g * BLK, BLK), :],
                                 ACT.Copy).then_inc(be_stage, 1)
                    act.wait_ge(be_stage, m * BPB + (g + 1))
                    for q in range(BLK // QUAD):
                        t = half * BLK + q * QUAD
                        quads = m * (P // QUAD) + (g * (BLK // QUAD) + q)
                        act.wait_ge(ta_ps, quads + 2)
                        a.activation(da[:, t:t + QUAD, :].rearrange("p t d -> p (t d)"), ps[q % 2][:, :], ACT.Exp, scale=16.0)\
                            .then_inc(exp_done, 1)
                        act.wait_ge(tu_ps, quads + 1)
                        for j in range(QUAD):
                            last = a.activation(ur[:, t + j, :], ps[2][:, j * P:(j + 1) * P], ACT.Copy,
                                                scale=ring_be[:, t + j, 0:1])
                        last.then_inc(u_done, 1)
                    y_out_of_psum(m * BPB + g)
                    for kind, i, j, _ in by_block[g]:
                        if kind == "up":
                            if j == 0:
                                act.wait_ge(mm2_ps, m * (TPE * 2) + (i * 2 + 1))
                            act.wait_ge(mm1_ps, m * (TPE * FC // 2) + (i * FC // 2 + j + 2))
                            a.activation(hid[:, 2 * j:2 * j + 2, :].rearrange("p c s -> p (c s)"), ps[4 + j % 2][:, :],
                                         ACT.Gelu).then_inc(gelu_done, 1)
                        elif kind == "turn":
                            act.wait_ge(xt_tp, m * TPE + (i + 2))
                            a.activation(xt.rearrange("p k s -> p (k s)"), ps[6][:, :], ACT.Copy).then_inc(xt_in, 1)
                        elif j == 1:
                            act.wait_ge(mm2_ps, m * (TPE * 2) + (i * 2 + 3))
                            act.wait_ge(ye_out, m * (16 * TPE) + (i * 16 + 1))
                            a.activation(yrow.rearrange("p c d -> p (c d)"), ps[7][:, :], ACT.Copy).then_inc(ye_sb, 1)
                    f = g // 4
                    if g % 4 == 0:
                        act.wait_ge(stage_in, m * 32 + (16 * (f + 2)))
                        act.wait_ge(ta_ps, m * (P // QUAD) + (f * (HALF // QUAD) + 1))
                    last = tanh_ops(1 - f, 8 * (g % 4), 8)
                    if g % 4 == 3:
                        last.then_inc(tanh_done, 1)
            for n in range(NBLK, NBLK + 2):
                y_out_of_psum(n)
            for i in range(CH):
                act.wait_ge(f_ready, NB * (i + 1))
                if i >= 2:
                    act.wait_ge(o_ready, i - 1)
                a.activation(sl[:, i % 2], fm[:, i % 2], ACT.Silu).then_inc(silu_done, 1)

        @block.tensor
        def _(pe):
            t = nc.tensor
            pe.wait_ge(consts, CONSTS)
            pe.wait_ge(ld_w, 64)
            for i in range(CH):
                pe.wait_ge(xn_ready, i + 1)
                if i >= 1:
                    pe.wait_ge(xt_sb, i)
                for k in range(DH):
                    for b in range(NB):
                        last = t.transpose(ps[k][:, b * P:(b + 1) * P], xnat[:, b, i, k * P:(k + 1) * P], ident[:, :])
                last.then_inc(xt_ps, 1)
                pe.wait_ge(xt_sb, i + 1)
                if i >= 1:
                    pe.wait_ge(z_used, i)
                for h in range(DH):
                    for k in range(DH):
                        last = t.matmul(ps[2 + h][:, :], wdt_sb[:, k, h * P:(h + 1) * P],
                                        xnT[:, i, k].rearrange("p b t -> p (b t)"), start=k == 0, stop=k == DH - 1)
                last.then_inc(z_ps, 1)
                if i >= 1:
                    pe.wait_ge(bc_sb, i)
                for w, sbw in enumerate((wb_sb, wc_sb)):
                    for b in range(NB):
                        for k in range(DH):
                            last = t.matmul(ps[4][32 * b:32 * b + 32, w * P:(w + 1) * P], sbw[:, k, :], xnT[:, i, k, b, :],
                                            start=k == 0, stop=k == DH - 1)
                last.then_inc(bc_ps, 1)
                for b in range(NB):
                    j = b * CH + i
                    for k in range(DH):
                        last = t.matmul(ps[6][:, j * NE:(j + 1) * NE], xnT[:, i, k, b, :], wg_sb[:, k, :],
                                        start=k == 0, stop=k == DH - 1)
                if i == CH - 1:
                    last.then_inc(lg_ps, 1)
            pe.wait_ge(rt_in, 1)
            flat = ohb.rearrange("p e k j -> p (e k j)")
            t.matmul(ps[7][:, :], lows, flat, start=True, stop=True)
            t.matmul(ps[6][:, :], ones[:, :], flat, start=True, stop=True).then_inc(rank_ps, 1)
            for i in range(CH):
                pe.wait_ge(sq_ready, i + 1)
                if i >= 1:
                    pe.wait_ge(e_used, i)
                for b in range(NB):
                    for k in range(DH):
                        t.matmul(ps[5][32 * b:32 * b + 32, 0:P], ones[:, 0:32], sq[:, k, b * P:(b + 1) * P],
                                 start=k == 0, stop=k == DH - 1)
                pe.wait_ge(sqb_ready, i + 1)
                t.matmul(ps[5][:, P:2 * P], bsum[:, :], sqb, start=True, stop=True).then_inc(e_ps, 1)
            pe.wait_ge(e_ps, CH)
            pe.sem_inc(loop_go, 1)
            pe.wait_ge(loop_go, 5)
            pe.sem_inc(mm1_ps, 1)
            pe.sem_inc(mm2_ps, 1)
            pe.sem_inc(y_done, 1)
            pe.sem_inc(ta_ps, 1)

            def turn_rows(n):
                for k in range(DH):
                    for c in range(2):
                        last = t.transpose(ps[6][:, k * TS + c * P:k * TS + (c + 1) * P], xrow[:, c, k * P:(k + 1) * P], ident[:, :])
                return last

            pe.wait_ge(xrow_in, 16)
            turn_rows(0).then_inc(xt_tp, 1)

            def turn_inputs(f, block_):
                c = block_ * P
                return t.transpose(ps[3][:, P:2 * P], stage[:, f, 1, c:c + P], ident[:, :])

            pe.wait_ge(stage_in, 16)
            turn_inputs(0, 0).then_inc(x0_ps, 1)

            def output(n, count):
                pe.wait_ge(win_ready, n + 1)
                pe.wait_ge(h_ready, count)
                pe.wait_ge(dx_in, (n + 1) * 16)
                pe.wait_ge(y_sb, n + 1)

            def output_products(half, following):
                if following is not None:
                    turn_inputs(*following)
                t.matmul(ps[3][:, 0:P], ident[:, :], dxt, start=True, stop=False)
                for j in range(BLK):
                    last = t.matmul(ps[3][:, 0:P], win[:, j, BLK - 1 - j:2 * BLK - 1 - j, :].rearrange("p c g -> p (c g)"), hr[:, half * BLK + j, :],
                                    start=False, stop=j == BLK - 1)
                last.then_inc(y_done, 1)

            pe.wait_ge(h_ready, BLK + 1)
            with pe.Fori(0, CH) as m:
                for g in range(BPB):
                    f = g // 4
                    if g % 4 == 0:
                        pe.wait_ge(tanh_done, m * 2 + (f + 1))
                        pe.wait_ge(stage_in, m * 32 + 16 * (f + 1))
                    for q in range(BLK // QUAD):
                        quads = m * (P // QUAD) + (g * (BLK // QUAD) + q)
                        pe.wait_ge(exp_done, quads + 1)
                        for j in range(QUAD):
                            s = (g % 4) * BLK + q * QUAD + j
                            last = t.transpose(ps[q % 2][:, j * P:(j + 1) * P], tanhb[:, f, :, s], ident[:, :])
                        last.then_inc(ta_ps, 1)
                        pe.wait_ge(u_done, quads + 1)
                        if q == 0:
                            pe.wait_ge(y_sb, m * BPB + (g + 1))
                        for j in range(QUAD):
                            last = t.matmul(ps[2][:, j * P:(j + 1) * P], pick[:, q * QUAD + j, :], yx[:, 1, :], start=True, stop=True)
                        last.then_inc(tu_ps, 1)
                    output(m * BPB + g, m * P + (g * BLK + 1))
                    if g % 4 == 3:
                        pe.wait_ge(stage_in, m * 32 + 16 * (f + 2))
                    output_products(g % 2, ((g + 1) // 4 % 2, (g + 1) % 4))
                    for kind, i, j, _ in by_block[g]:
                        if kind == "up":
                            if j == 0:
                                if i == 0:
                                    pe.wait_ge(wf_in, m * 16 + 16)
                                pe.wait_ge(xt_in, m * TPE + (i + 1))
                            pe.wait_ge(gelu_done, m * (TPE * FC // 2) + (i * FC // 2 + j + 1))
                            for c in range(2):
                                for k in range(DH):
                                    last = t.matmul(ps[4 + j % 2][:, c * TS:(c + 1) * TS],
                                                    wf[:, k, (2 * j + c) * P:(2 * j + c + 1) * P], xt[:, k, :],
                                                    start=k == 0, stop=k == DH - 1)
                            last.then_inc(mm1_ps, 1)
                        elif kind == "turn":
                            pe.wait_ge(xrow_in, m * (16 * TPE) + 16 * (i + 2))
                            turn_rows(i + 1).then_inc(xt_tp, 1)
                        else:
                            if j == 0:
                                if i == 0:
                                    pe.wait_ge(wp_in, m * 16 + 16)
                                pe.wait_ge(gelu_done, m * (TPE * FC // 2) + ((i + 1) * FC // 2 + 2))
                                pe.wait_ge(ye_sb, m * TPE + (i + 1))
                            for k in range(FC):
                                last = t.matmul(ps[7][:, j * D:(j + 1) * D], hid[:, k, j * P:(j + 1) * P], wp[:, k, :],
                                                start=k == 0, stop=k == FC - 1)
                            last.then_inc(mm2_ps, 1)
            for n in range(NBLK, NBLK + 2):
                output(n, (n - 1) * BLK + BLK + 1)
                output_products(n % 2, None)


def kernel(**inputs):
    import numpy as _np
    import concourse.bacc as _bacc
    from concourse import mybir as _mybir
    from concourse.bass_utils import run_bass_kernel_spmd as _run

    def state_columns(w):
        wt = _np.transpose(w)
        return _np.ascontiguousarray(_np.concatenate([wt] * DH, axis=1))

    laid = {
        "x": inputs["L0_attn_x"],
        "wdtT": _np.ascontiguousarray(_np.transpose(inputs["L0_attn_Wdt"])),
        "bdt": inputs["L0_attn_bdt"],
        "wb": state_columns(inputs["L0_attn_WB"]),
        "wc": state_columns(inputs["L0_attn_WC"]),
        "a_log": inputs["L0_attn_A_log"],
        "dpar": inputs["L0_attn_Dp"],
        "w_g": inputs["L0_ffn_w_g"],
        "c_fc": inputs["L0_ffn_c_fc"],
        "c_proj": inputs["L0_ffn_c_proj"],
    }
    nc = _bacc.Bacc("TRN2", target_bir_lowering=False, num_devices=1)
    arrays, args = {}, []
    for name, a in laid.items():
        a = _np.ascontiguousarray(a)
        arrays[f"in_{name}"] = a
        args.append(nc.dram_tensor(f"in_{name}", a.shape, _mybir.dt.from_np(a.dtype), kind="ExternalInput").ap())
    out = nc.dram_tensor("out_0", (NB, NT, D), _mybir.dt.float32, kind="ExternalOutput").ap()
    build(nc, *args, out)
    r = _run(nc, [arrays], core_ids=[0])
    return r.results[0]["out_0"]
```

```python
from contextlib import ExitStack

import concourse.bass as bass
from concourse import mybir

NB, NT, D, NS = 4, 1024, 256, 16
NE, CAP, FF = 8, 1280, 1024
P = 128
DH = D // P
TOK = NB * NT
TILES = TOK // P
CH = NT // P
HALF = 64
NHALF = NT // HALF
BLK = 16
NBLK = NT // BLK
BPB = P // BLK
QUAD = 4
QPB = BLK // QUAD
RING = 2 * BLK
SLOTS = NE * CAP
TS = 256
TPE = CAP // TS
PADROWS = 2 * TS
TRASH = SLOTS + PADROWS
XE_ROWS = TRASH + 2 * TOK
YPAD = 2 * BLK
FC = FF // P
CLAMP = 20.0
DT_LO, DT_HI, SHARP = 0.001, 0.1, 0.5
DT_C, DT_R = (DT_HI + DT_LO) / 2, (DT_HI - DT_LO) / 2
WIN = 2 * BLK - 1
NG = NB * DH
TURN_BANKS = ((0, 1), (5, 7))
CONSTS = 20


def build(nc, x, wdtT, bdt, wb, wc, a_log, dpar, w_g, c_fc, c_proj, out):
    f32, bf16, i32 = mybir.dt.float32, mybir.dt.bfloat16, mybir.dt.int32
    ALU, ACT, AX = mybir.AluOpType, mybir.ActivationFunctionType, mybir.AxisListType
    ctx = ExitStack()
    with ctx:
        def sb(name, shape, dt=f32):
            return ctx.enter_context(nc.sbuf_tensor(name, shape, dt))

        def sem(name):
            return ctx.enter_context(nc.semaphore(name))

        xe = nc.dram_tensor("xe", (XE_ROWS, D), f32, kind="Internal").ap()
        ye = nc.dram_tensor("ye", (SLOTS, D), f32, kind="Internal").ap()
        feed = nc.dram_tensor("feed", (NHALF + 1, P, 2, NB * DH * HALF), f32, kind="Internal").ap()
        dx = nc.dram_tensor("dx", (NT + YPAD, NB, D), f32, kind="Internal").ap()
        ys = nc.dram_tensor("ys", (NT + YPAD, NB, D), f32, kind="Internal").ap()

        ident = sb("ident", [P, P])
        ones = sb("ones", [P, P])
        bsum = sb("bsum", [P, P])
        winmask = sb("winmask", [P, 8])
        zeros = sb("zeros", [P, 2 * D])
        neghalf = sb("neghalf", [P, NB])
        pick = sb("pick", [P, BLK, P])
        dtbias = sb("dtbias", [P, 1])
        a16 = sb("a16", [P, DH * NS])
        be = sb("be", [P, NT, 2])
        ccol = sb("ccol", [P, BLK + NT])
        mv = sb("mv", [P, TILES, 2])
        rstd = sb("rstd", [P, TILES])
        wsel = sb("wsel", [P, 2, TILES])
        src_i = sb("src_i", [P, 2, TILES], i32)
        dst_i = sb("dst_i", [P, 2, TILES], i32)

        ARENA = 40704
        arena = sb("arena", [P, ARENA])
        at = [0]

        def take(n):
            at[0] += n
            assert at[0] <= ARENA, at[0]
            return arena[:, at[0] - n:at[0]]

        SD = NB * DH * HALF
        tanhb = take(2 * P * HALF).rearrange("p (f s t) -> p f s t", f=2, t=HALF)
        stage = take(2 * 2 * SD).rearrange("p (f w s) -> p f w s", f=2, w=2)
        da = take(RING * P).rearrange("p (t d) -> p t d", d=P)
        ur = take(RING * P).rearrange("p (t d) -> p t d", d=P)
        hr = take(RING * P).rearrange("p (t d) -> p t d", d=P)
        win = take(BLK * NG * WIN).rearrange("p (t c g) -> p t c g", g=NG, c=WIN)
        xt = take(DH * TS).rearrange("p (k s) -> p k s", k=DH)
        hid = take(FC * TS).rearrange("p (k s) -> p k s", k=FC)
        xrow = take(2 * D).rearrange("p (c d) -> p c d", c=2)
        yrow = take(2 * D).rearrange("p (c d) -> p c d", c=2)
        wf = sb("wf", [P, DH, FF])
        wp = sb("wp", [P, FC, D])
        ysb = take(P)
        xin = take(P)
        dxt = take(P)
        vv = take(P)
        junk = take(2 * P).rearrange("p (f d) -> p f d", f=2)
        junkq = take(64)
        ac = take(2)
        tr = take(64)
        qv = take(1)
        mx = take(1)
        sv = take(RING * 2).rearrange("p (t w) -> p t w", w=2)
        cs = take(BLK)
        ring_be = take(RING * 2).rearrange("p (t w) -> p t w", w=2)

        at2 = [0]

        def lay(n):
            at2[0] += n
            assert at2[0] <= ARENA, at2[0]
            return arena[:, at2[0] - n:at2[0]]

        xnat = lay(TILES * D).rearrange("p (b i d) -> p b i d", b=NB, i=CH)
        xnT = lay(CH * DH * NB * P).rearrange("p (i k b t) -> p i k b t", i=CH, k=DH, b=NB)
        spl = lay(CH * DH * NB * P).rearrange("p (i k m) -> p i k m", i=CH, k=DH)
        rel = lay(2 * DH * NB * P).rearrange("p (f k m) -> p f k m", f=2, k=DH)
        dtc = lay(2 * 2 * SD).rearrange("p (f s) -> p f s", f=2)
        dxc = lay(2 * 2 * SD).rearrange("p (f s) -> p f s", f=2)
        sq = lay(DH * NB * P).rearrange("p (k m) -> p k m", k=DH)
        sqb = lay(P)
        dsb = lay(P)
        dxn = lay(2 * NB * D).rearrange("p (f b d) -> p f b d", f=2, b=NB)
        wdt_sb = lay(DH * D).rearrange("p (k m) -> p k m", k=DH)
        wb_sb = lay(DH * 32).rearrange("p (k m) -> p k m", k=DH)
        wc_sb = lay(DH * 32).rearrange("p (k m) -> p k m", k=DH)
        wg_sb = lay(DH * NE).rearrange("p (k m) -> p k m", k=DH)
        dpb = lay(D)
        bdt_sb = lay(DH)
        stats = lay(2 * NB * 6).rearrange("p (f b s) -> p f b s", f=2, b=NB)
        vare = lay(CH * NB).rearrange("p (i b) -> p i b", i=CH)
        JT = TILES
        lg = lay(NE * JT).rearrange("p (e j) -> p e j", e=NE)
        lgw = lay(NE * JT).rearrange("p (e j) -> p e j", e=NE)
        iom = lay(NE * JT).rearrange("p (e j) -> p e j", e=NE)
        iom_i = lay(NE * JT).bitcast(i32).rearrange("p (e j) -> p e j", e=NE)
        tmp = lay(NE * JT).rearrange("p (e j) -> p e j", e=NE)
        ohb = lay(NE * 2 * JT).rearrange("p (e k j) -> p e k j", e=NE, k=2)
        ohf = lay(NE * 2 * JT).rearrange("p (e k j) -> p e k j", e=NE, k=2)
        rkt = lay(NE * 2 * JT).rearrange("p (e k j) -> p e k j", e=NE, k=2)
        tot = lay(NE * 2 * JT).rearrange("p (e k j) -> p e k j", e=NE, k=2)
        inc = lay(NE * 2 * JT).rearrange("p (e k j) -> p e k j", e=NE, k=2)
        keepm = lay(NE * 2 * JT).rearrange("p (e k j) -> p e k j", e=NE, k=2)
        lows = lay(P)
        top = lay(2 * JT).rearrange("p (k j) -> p k j", k=2)
        eix = lay(2 * JT).rearrange("p (k j) -> p k j", k=2)
        rank = lay(2 * JT).rearrange("p (k j) -> p k j", k=2)
        keep = lay(2 * JT).rearrange("p (k j) -> p k j", k=2)
        row = lay(2 * JT).rearrange("p (k j) -> p k j", k=2)
        trash = lay(2 * JT).rearrange("p (k j) -> p k j", k=2)
        trash_i = lay(2 * JT).bitcast(i32).rearrange("p (k j) -> p k j", k=2)
        pw = lay(4 * JT).rearrange("p (k j) -> p k j", k=4)
        alog = lay(DH * NS)
        prologue_words = at2[0]

        at3 = [0]

        def end(n):
            at3[0] += n
            assert at3[0] <= ARENA, at3[0]
            return arena[:, at3[0] - n:at3[0]]

        GR = 4
        xl = end(2 * GR * D).rearrange("p (f g d) -> p f g d", f=2, g=GR)
        yl = end(2 * GR * D).rearrange("p (f g d) -> p f g d", f=2, g=GR)
        g0 = end(2 * GR * D).rearrange("p (f g d) -> p f g d", f=2, g=GR)
        g1 = end(2 * GR * D).rearrange("p (f g d) -> p f g d", f=2, g=GR)
        fm = end(2 * GR * D).rearrange("p (f g d) -> p f g d", f=2, g=GR)
        sl = end(2 * GR * D).rearrange("p (f g d) -> p f g d", f=2, g=GR)
        ol = end(2 * GR * D).rearrange("p (f g d) -> p f g d", f=2, g=GR)

        ps = [ctx.enter_context(nc.psum_tensor(f"ps{i}", [P, 512], f32)) for i in range(8)]

        ld_x = [sem(f"ld_x{k}") for k in range(CH)]
        ld_w = sem("ld_w")
        ld_v = sem("ld_v")
        memz = sem("memz")
        padz = sem("padz")
        consts = sem("consts")
        stat_chain = sem("stat_chain")
        stat_ready = sem("stat_ready")
        rstd_ready = sem("rstd_ready")
        xn_ready = sem("xn_ready")
        xt_ps = sem("xt_ps")
        xt_sb = sem("xt_sb")
        z_ps = sem("z_ps")
        z_used = sem("z_used")
        act_chain = sem("act_chain")
        sp_half = sem("sp_half")
        sp_ready = sem("sp_ready")
        th_ready = sem("th_ready")
        bc_ps = sem("bc_ps")
        bc_sb = sem("bc_sb")
        sq_ready = sem("sq_ready")
        sqb_ready = sem("sqb_ready")
        e_ps = sem("e_ps")
        e_chain = sem("e_chain")
        e_used = sem("e_used")
        dt_ready = sem("dt_ready")
        fst_ready = sem("fst_ready")
        fst_done = [sem(f"fst_done{k}") for k in range(2)]
        dxn_ready = sem("dxn_ready")
        dx_done = [sem(f"dx_done{k}") for k in range(2)]
        lg_ps = sem("lg_ps")
        rt_in = sem("rt_in")
        rank_ps = sem("rank_ps")
        rt_chain = sem("rt_chain")
        gap_ready = sem("gap_ready")
        gap_exp = sem("gap_exp")
        route_ready = sem("route_ready")
        a_tanh = sem("a_tanh")
        a_exp = sem("a_exp")
        a_ready = sem("a_ready")
        scat_done = sem("scat_done")
        loop_go = sem("loop_go")
        init_win = sem("init_win")
        T_ready = sem("T_ready")
        h_ready = sem("h_ready")
        q_ready = sem("q_ready")
        v_ready = sem("v_ready")
        m_ready = sem("m_ready")
        s_ready = sem("s_ready")
        ac_ready = sem("ac_ready")
        ta_ps = sem("ta_ps")
        da_done = sem("da_done")
        tu_ps = sem("tu_ps")
        u_done = sem("u_done")
        be_stage = sem("be_stage")
        tanh_done = sem("tanh_done")
        stage_in = sem("stage_in")
        cs_ready = sem("cs_ready")
        win_ready = sem("win_ready")
        y_done = sem("y_done")
        y_sb = sem("y_sb")
        x_ps = sem("x_ps")
        x_sb = sem("x_sb")
        decay_ready = sem("decay_ready")
        y_out = sem("y_out")
        dx_in = sem("dx_in")
        xrow_in = sem("xrow_in")
        xt_tp = sem("xt_tp")
        xt_in = sem("xt_in")
        mm1_ps = sem("mm1_ps")
        gelu_done = sem("gelu_done")
        mm2_ps = sem("mm2_ps")
        ye_sb = sem("ye_sb")
        ye_out = sem("ye_out")
        wf_in = sem("wf_in")
        wp_in = sem("wp_in")
        fin_x = [sem(f"fin_x{k}") for k in range(2)]
        fin_y = [sem(f"fin_y{k}") for k in range(2)]
        fin_g = [sem(f"fin_g{k}") for k in range(2)]
        f_half = sem("f_half")
        f_ready = sem("f_ready")
        silu_done = sem("silu_done")
        f_mul = sem("f_mul")
        o_ready = sem("o_ready")
        o_out = [sem(f"o_out{k}") for k in range(2)]

        xn_tok = x.rearrange("b (i p) d -> p b i d", p=P)
        dx_tok = dx[YPAD:].rearrange("(i p) b d -> p i b d", p=P)
        ys_tok = ys[YPAD:].rearrange("(i p) b d -> p i b d", p=P)
        out_tok = out.rearrange("b (i p) d -> p b i d", p=P)

        work = []
        for i in range(TPE):
            work += [("up", i, j, 4) for j in range(FC // 2)] + [("turn", i, 0, 1)] + [("down", i, c, 8) for c in range(2)]
        total = sum(w[3] for w in work)
        by_quad, n = [[] for _ in range(P // QUAD)], 0
        for w in work:
            by_quad[min(P // QUAD - 1, (n + w[3] // 2) * (P // QUAD) // total)].append(w)
            n += w[3]

        block = ctx.enter_context(nc.Block())

        @block.sync
        def _(sp):
            for i in range(CH):
                sp.dma_start(xnat[:, :, i, :], xn_tok[:, :, i, :]).then_inc(ld_x[i], 16)
            sp.dma_start(wdt_sb, wdtT.rearrange("(k p) m -> p k m", p=P)).then_inc(ld_w, 16)
            sp.dma_start(wb_sb, wb.rearrange("(k p) m -> p k m", p=P)).then_inc(ld_w, 16)
            sp.dma_start(wc_sb, wc.rearrange("(k p) m -> p k m", p=P)).then_inc(ld_w, 16)
            sp.dma_start(wg_sb, w_g.rearrange("(k p) m -> p k m", p=P)).then_inc(ld_w, 16)
            sp.dma_start(bdt_sb, bdt.rearrange("(k p) -> p k", p=P), allow_slow_non_contiguous=True).then_inc(ld_v, 16)
            sp.dma_start(alog.rearrange("p (k n) -> p k n", k=DH), a_log.rearrange("(k p) n -> p k n", p=P)).then_inc(ld_v, 16)
            sp.dma_start(dpb, dpar.rearrange("(a d) -> a d", a=1).broadcast_to([P, D])).then_inc(ld_v, 16)
            sp.wait_ge(memz, 1)
            sp.dma_start(xe[0:TRASH, :].rearrange("(r p) d -> p r d", p=P),
                         zeros[:, 0:D].unsqueeze(1).broadcast_to([P, TRASH // P, D])).then_inc(padz, 16)
            for b in range(NB):
                sp.dma_start(dx[0:YPAD, b, :], zeros[0:YPAD, 0:D]).then_inc(padz, 16)
            for i in range(CH):
                sp.wait_ge(dxn_ready, i + 1)
                sp.dma_start(dx_tok[:, i], dxn[:, i % 2]).then_inc(dx_done[i % 2], 16)
            for i in range(CH):
                sp.wait_ge(fst_ready, i + 1)
                for h in range(2):
                    sp.dma_start(feed[2 * i + h, :, 0, :].rearrange("p (g t) -> p g t", t=HALF),
                                 dtc[:, i % 2].rearrange("p (g h t) -> p h g t", h=2, t=HALF)[:, h]).then_inc(fst_done[i % 2], 16)
                sp.dma_start(feed[2 * i:2 * i + 2, :, 1, :].rearrange("h p s -> p h s"),
                             dxc[:, i % 2].rearrange("p (h s) -> p h s", h=2)).then_inc(fst_done[i % 2], 16)
            sp.dma_start(feed[NHALF, :, 0, :], dtc[:, 1, 0:SD]).then_inc(fst_done[0], 16)
            sp.dma_start(feed[NHALF, :, 1, :], dxc[:, 1, 0:SD]).then_inc(fst_done[0], 16)
            sp.wait_ge(fst_done[0], 48 * CH // 2 + 32)
            sp.wait_ge(fst_done[1], 48 * CH // 2)
            for k in range(2):
                sp.wait_ge(dx_done[k], 16 * CH // 2)
            sp.sem_inc(loop_go, 1)
            sp.wait_ge(loop_go, 5)
            sp.sem_inc(y_out, 1)
            sp.sem_inc(ye_out, 1)
            sp.dma_start(stage[:, 0, :, :], feed[0]).then_inc(stage_in, 16)
            sp.dma_start(xrow, xe[0:TS, :].rearrange("(c p) d -> p c d", p=P)).then_inc(xrow_in, 16)
            sp.wait_ge(xt_tp, 1)
            sp.dma_start(xrow, xe[TS:2 * TS, :].rearrange("(c p) d -> p c d", p=P)).then_inc(xrow_in, 16)

            def load_dx(n, at):
                sp.wait_ge(y_done, n + 1)
                sp.dma_start(dxt, dx[at, :, :].rearrange("t b (k d) -> (t b k) d", k=DH)).then_inc(dx_in, 16)

            def store_y(n, at):
                sp.wait_ge(y_sb, n + 1)
                sp.dma_start(ys[at, :, :].rearrange("t b (k d) -> (t b k) d", k=DH), ysb).then_inc(y_out, 16)

            def experts_rows(m, kind, i, j):
                if kind == "turn":
                    sp.wait_ge(xt_tp, m * TPE + i + 2)
                    sp.dma_start(xrow, xe[bass.ds(m * CAP + (i + 2) * TS, TS), :]
                                 .rearrange("(c p) d -> p c d", p=P)).then_inc(xrow_in, 16)
                if kind == "down" and j == 1:
                    sp.wait_ge(ye_sb, m * TPE + i + 2)
                    sp.dma_start(ye[bass.ds(m * CAP + i * TS, TS), :]
                                 .rearrange("(c p) d -> p c d", p=P), yrow).then_inc(ye_out, 16)

            with sp.Fori(0, CH) as m:
                sp.wait_ge(mm1_ps, m * (TPE * FC // 2) + 1)
                sp.dma_start(wf[:, :, :], c_fc[bass.ds(m, 1), :, :].rearrange("e (k p) f -> p (e k) f", p=P)).then_inc(wf_in, 16)
                sp.wait_ge(mm2_ps, m * (TPE * 2) + 1)
                sp.dma_start(wp[:, :, :], c_proj[bass.ds(m, 1), :, :].rearrange("e (k p) d -> p (e k) d", p=P)).then_inc(wp_in, 16)
                for g in range(BPB):
                    if g % 4 == 0:
                        f = g // 4
                        sp.wait_ge(tanh_done, m * 2 + f + 1)
                        sp.dma_start(stage[:, 1 - f, :, :].rearrange("p w s -> p (w s)"),
                                     feed[bass.ds(m * 2 + f + 1, 1), :, :, :].rearrange("h p w s -> p (h w s)")).then_inc(stage_in, 16)
                    load_dx(m * BPB + g, bass.ds(m * P + g * BLK, BLK))
                    for kind, i, j, _ in sum(by_quad[g * QPB:g * QPB + 2], []):
                        experts_rows(m, kind, i, j)
                    store_y(m * BPB + g, bass.ds(m * P + g * BLK, BLK))
                    for kind, i, j, _ in sum(by_quad[g * QPB + 2:(g + 1) * QPB], []):
                        experts_rows(m, kind, i, j)
            for n in range(NBLK, NBLK + 2):
                load_dx(n, slice(n * BLK, (n + 1) * BLK))
                store_y(n, slice(n * BLK, (n + 1) * BLK))
            sp.wait_ge(decay_ready, NHALF + 1)
            sp.wait_ge(ta_ps, NT // QUAD + 1)
            sp.wait_ge(y_out, 16 * (NBLK + 2) + 1)
            for i in range(CH):
                if i >= 2:
                    sp.wait_ge(o_ready, i - 1)
                sp.dma_start(xl[:, i % 2], xn_tok[:, :, i, :]).then_inc(fin_x[i % 2], 16)
                sp.dma_start(yl[:, i % 2], ys_tok[:, i]).then_inc(fin_y[i % 2], 16)
                if i >= 1:
                    sp.wait_ge(o_ready, i)
                    sp.dma_start(out_tok[:, :, i - 1, :], ol[:, (i - 1) % 2]).then_inc(o_out[(i - 1) % 2], 16)
            sp.wait_ge(o_ready, CH)
            sp.dma_start(out_tok[:, :, CH - 1, :], ol[:, (CH - 1) % 2]).then_inc(o_out[(CH - 1) % 2], 16)
            for k in range(2):
                sp.wait_ge(o_out[k], 16 * CH // 2)
            sp.wait_ge(padz, 16 * (NB + 1))
            sp.wait_ge(ye_out, 16 * NE * TPE + 1)

        @block.gpsimd
        def _(pool):
            g = nc.gpsimd
            n = [0]

            def made(ins):
                n[0] += 1
                ins.then_inc(consts, 1)

            g.memset(zeros[:, :], 0.0).then_inc(memz, 1)
            made(g.memset(ident[:, :], 0.0))
            made(g.memset(ones[:, :], 1.0))
            made(g.memset(pick[:, :, :], 0.0))
            made(g.memset(bsum[:, :], 0.5))
            made(g.memset(winmask[:, :], 1.0))
            made(g.memset(neghalf[:, :], -0.5))
            made(g.memset(dtbias[:, :], -DT_C * SHARP / (DT_R + 1e-8)))
            made(g.memset(lows, 1.0))
            made(g.memset(keepm, 1.0))
            made(g.memset(ccol[:, 0:BLK], 0.0))
            made(g.iota(iom_i, pattern=[[1, NE], [0, JT]], base=-NE, channel_multiplier=0))
            made(g.iota(trash_i, pattern=[[TOK, 2], [P, JT]], base=TRASH, channel_multiplier=1))
            pool.wait_ge(consts, n[0])
            made(g.affine_select(out=ident[:, :], in_=ident[:, :], compare_op=ALU.not_equal, fill=1.0, base=0,
                                 pattern=[[-1, P]], channel_multiplier=1))
            pk = pick[:, :, :].rearrange("p t (g n) -> p t g n", g=NG)
            made(g.affine_select(out=pk, in_=pk, compare_op=ALU.not_equal, fill=1.0, base=0,
                                 pattern=[[-NG, BLK], [-1, NG], [0, NS]], channel_multiplier=1))
            q4 = bsum[:, :].rearrange("p (b c) -> p b c", b=NB)
            made(g.affine_select(out=q4, in_=q4, compare_op=ALU.is_ge, fill=0.0, base=0,
                                 pattern=[[-32, NB], [0, 32]], channel_multiplier=1))
            made(g.affine_select(out=winmask[:, :], in_=winmask[:, :], compare_op=ALU.is_ge, fill=0.0, base=0,
                                 pattern=[[-NS, NG]], channel_multiplier=1))
            made(g.affine_select(out=lows, in_=lows, compare_op=ALU.is_gt, fill=0.0, base=0,
                                 pattern=[[1, P]], channel_multiplier=-1))
            made(g.memset(keepm[:, :, 0, 0:1], 0.0))
            pool.wait_ge(consts, n[0])
            made(g.affine_select(out=q4, in_=q4, compare_op=ALU.is_ge, fill=0.0, base=31,
                                 pattern=[[32, NB], [0, 32]], channel_multiplier=-1))
            made(g.affine_select(out=winmask[:, :], in_=winmask[:, :], compare_op=ALU.is_ge, fill=0.0, base=NS - 1,
                                 pattern=[[NS, NG]], channel_multiplier=-1))
            assert n[0] == CONSTS, n[0]
            rs = rstd[:, :].rearrange("p (b i) -> p b i", b=NB)
            for i in range(CH + 3):
                if i < CH:
                    pool.wait_ge(stat_ready, i + 1)
                    g.tensor_tensor(rs[:, :, i], vare[:, i, :], neghalf[:, :], ALU.pow).then_inc(rstd_ready, 1)
                if i >= 3:
                    c = i - 3
                    pool.wait_ge(sp_half, c + 1)
                    g.tensor_tensor(spl[:, c], spl[:, c], rel[:, c % 2], ALU.add).then_inc(sp_ready, 1)
            pool.wait_ge(padz, 16 * (NB + 1))
            pool.wait_ge(route_ready, 1)
            pool.wait_ge(xn_ready, CH)
            for b in range(NB):
                for i in range(CH):
                    for k in range(2):
                        g.indirect_dma_start(
                            out=xe, out_offset=bass.IndirectOffsetOnAxis(ap=dst_i[:, k, b * CH + i:b * CH + i + 1], axis=0),
                            in_=xnat[:, b, i, :], in_offset=None,
                            bounds_check=XE_ROWS - 1, oob_is_err=True).then_inc(scat_done, 16)
            pool.wait_ge(scat_done, 16 * 2 * TILES)
            pool.sem_inc(loop_go, 1)
            pool.wait_ge(loop_go, 5)
            g.memset(win, 0.0).then_inc(init_win, 1)
            g.memset(sv, 1.0).then_inc(init_win, 1)
            pool.wait_ge(init_win, 2)
            pool.sem_inc(win_ready, 1)
            pool.sem_inc(s_ready, BLK)

            def scale_of(slot, count):
                pool.wait_ge(m_ready, count)
                g.tensor_tensor(sv[:, slot, 1:2], mx, neghalf[:, 0:1], ALU.pow).then_inc(s_ready, 1)

            def windows(half, ccols, count, blk):
                pool.wait_ge(s_ready, count)
                g.tensor_tensor(cs, ccols, sv[:, half * BLK:(half + 1) * BLK, 1], ALU.mult).then_inc(cs_ready, 1)
                pool.wait_ge(cs_ready, blk)
                pool.wait_ge(y_done, blk + 1)
                g.tensor_tensor(win[:, :, BLK - 1, :], cs.unsqueeze(2).broadcast_to([P, BLK, NG]),
                                winmask[:, :].unsqueeze(1).broadcast_to([P, BLK, NG]), ALU.mult).then_inc(win_ready, 1)

            with pool.Fori(0, NT // RING) as r:
                for k in range(RING):
                    scale_of((k - 1) % RING, r * RING + (k + 1 + BLK))
                    if k % BLK == 0:
                        windows(1 - k // BLK, ccol[:, bass.ds(r * RING + k, BLK)], r * RING + (k + 1 + BLK), r * 2 + (k // BLK + 1))
            scale_of(RING - 1, NT + 1 + BLK)
            windows(1, ccol[:, NT:NT + BLK], NT + 1 + BLK, NBLK + 1)
            pool.wait_ge(ye_out, 16 * NE * TPE + 1)
            pool.wait_ge(decay_ready, NHALF + 1)
            pool.wait_ge(ta_ps, NT // QUAD + 1)
            for i in range(CH):
                if i >= 2:
                    pool.wait_ge(f_ready, NB * (i - 1))
                for b in range(NB):
                    for k, to in enumerate((g0, g1)):
                        g.indirect_dma_start(
                            out=to[:, i % 2, b, :], out_offset=None, in_=ye,
                            in_offset=bass.IndirectOffsetOnAxis(ap=src_i[:, k, b * CH + i:b * CH + i + 1], axis=0),
                            bounds_check=SLOTS - 1, oob_is_err=True).then_inc(fin_g[i % 2], 16)

        @block.vector
        def _(dve):
            v = nc.vector

            links = [0]

            def link(ins):
                links[0] += 1
                ins.then_inc(stat_chain, 1)
                dve.wait_ge(stat_chain, links[0])

            mvt = mv[:, :, :].rearrange("p (b i) s -> p b i s", b=NB)

            def statistics(i):
                dve.wait_ge(ld_x[i], 16)
                for b in range(NB):
                    last = v.bn_stats(out=stats[:, i % 2, b, :], in_=xnat[:, b, i, :])
                link(last)
                for b in range(NB):
                    last = v.bn_aggr(out=mvt[:, b, i, :], in_=stats[:, i % 2, b, :])
                link(last)
                v.tensor_scalar(vare[:, i, :], mvt[:, :, i, 1], 1e-5, None, ALU.add).then_inc(stat_ready, 1)

            def normalize(i):
                dve.wait_ge(rstd_ready, i + 1)
                for b in range(NB):
                    j = b * CH + i
                    last = v.tensor_scalar(xnat[:, b, i, :], xnat[:, b, i, :], mv[:, j, 0:1], rstd[:, j:j + 1],
                                           ALU.subtract, ALU.mult)
                last.then_inc(xn_ready, 1)
                dve.wait_ge(xn_ready, i + 1)
                if i >= 2:
                    dve.wait_ge(dx_done[i % 2], 16 * (i // 2))
                v.tensor_tensor(dxn[:, i % 2, :, :], xnat[:, :, i, :], dpb.unsqueeze(1).broadcast_to([P, NB, D]),
                                ALU.mult).then_inc(dxn_ready, 1)

            def b_and_c(i):
                dve.wait_ge(bc_ps, i + 1)
                v.tensor_copy(be[:, i * P:(i + 1) * P, 0], ps[4][:, 0:P])
                v.tensor_copy(ccol[:, BLK + i * P:BLK + (i + 1) * P], ps[4][:, P:2 * P]).then_inc(bc_sb, 1)

            dve.wait_ge(ld_v, 48)
            statistics(0)
            for i in range(CH):
                if i + 1 < CH:
                    statistics(i + 1)
                normalize(i)
                if i >= 2:
                    b_and_c(i - 2)
            b_and_c(CH - 2)
            b_and_c(CH - 1)
            dve.wait_ge(consts, CONSTS)
            dve.wait_ge(a_exp, 1)
            v.tensor_scalar(a16[:, :], alog, -1.0 / 16.0, None, ALU.mult).then_inc(a_ready, 1)
            hops = [0]

            def hop(ins):
                hops[0] += 1
                ins.then_inc(rt_chain, 1)
                dve.wait_ge(rt_chain, hops[0])

            dve.wait_ge(lg_ps, 1)
            hop(v.tensor_copy(iom, iom_i))
            hop(v.tensor_copy(trash, trash_i))
            hop(v.tensor_copy(lg, ps[6][:, 0:NE * JT].rearrange("p (j e) -> p e j", e=NE)))
            for k in range(2):
                cur = lg if k == 0 else lgw
                hop(v.tensor_reduce(out=top[:, k, :], in_=cur.rearrange("p e j -> p j e"), axis=AX.X, op=ALU.max))
                hop(v.tensor_tensor(tmp, cur, top[:, k, :].unsqueeze(1).broadcast_to([P, NE, JT]), ALU.is_equal))
                hop(v.tensor_tensor(tmp, tmp, iom, ALU.mult))
                hop(v.tensor_reduce(out=eix[:, k, :], in_=tmp.rearrange("p e j -> p j e"), axis=AX.X, op=ALU.min))
                hop(v.tensor_tensor(ohf[:, :, k, :], iom, eix[:, k, :].unsqueeze(1).broadcast_to([P, NE, JT]), ALU.is_equal))
                if k == 0:
                    hop(v.scalar_tensor_tensor(lgw, ohf[:, :, 0, :], -3e38, lg, ALU.mult, ALU.add))
            v.tensor_tensor(pw[:, 0, :], top[:, 1, :], top[:, 0, :], ALU.subtract).then_inc(gap_ready, 1)
            v.tensor_copy(ohb, ohf).then_inc(rt_in, 1)
            dve.wait_ge(gap_exp, 1)
            hop(v.tensor_scalar(pw[:, 1, :], pw[:, 3, :], 1.0, None, ALU.add))
            hop(v.reciprocal(pw[:, 2, :], pw[:, 1, :]))
            hop(v.tensor_tensor(pw[:, 3, :], pw[:, 3, :], pw[:, 2, :], ALU.mult))
            dve.wait_ge(rank_ps, 1)
            kj = "p e k j -> p (e k j)"
            hop(v.tensor_copy(tot, ps[6][:, :].rearrange("p (e k j) -> p e k j", e=NE, k=2)))
            hop(v.tensor_tensor_scan(inc.rearrange(kj), keepm.rearrange(kj), tot.rearrange(kj), 0.0, ALU.mult, ALU.add))
            hop(v.tensor_tensor(inc, inc, tot, ALU.subtract))
            hop(v.tensor_tensor(inc, inc, ps[7][:, :].rearrange("p (e k j) -> p e k j", e=NE, k=2), ALU.add))
            hop(v.tensor_tensor(inc, inc, ohf, ALU.mult))
            hop(v.tensor_reduce(out=rank, in_=inc.rearrange("p e k j -> p k j e"), axis=AX.X, op=ALU.add))
            hop(v.tensor_scalar(keep, rank, float(CAP), None, ALU.is_lt))
            hop(v.tensor_scalar(row, eix, float(NE), float(CAP), ALU.add, ALU.mult))
            hop(v.tensor_tensor(row, row, rank, ALU.add))
            hop(v.tensor_tensor(rank, row, keep, ALU.mult))
            hop(v.tensor_copy(src_i[:, :, :], rank))
            hop(v.tensor_tensor(row, row, trash, ALU.subtract))
            hop(v.tensor_tensor(row, row, keep, ALU.mult))
            hop(v.tensor_tensor(row, row, trash, ALU.add))
            v.tensor_copy(dst_i[:, :, :], row)
            v.tensor_tensor(wsel[:, :, :], pw[:, 2:4, :], keep, ALU.mult).then_inc(route_ready, 1)

            def norm_of_input(i):
                cols = slice(i * P, (i + 1) * P)
                dve.wait_ge(e_ps, i + 1)
                v.tensor_copy(dsb, ps[5][:, P:2 * P]).then_inc(e_chain, 1)
                dve.wait_ge(e_chain, i + 1)
                v.scalar_tensor_tensor(be[:, cols, 1], ps[5][:, 0:P], 1.0 / CLAMP ** 2, dsb, ALU.mult, ALU.mult).then_inc(e_used, 1)

            dve.wait_ge(bc_sb, CH)
            for i in range(CH):
                dve.wait_ge(th_ready, i + 1)
                if i >= 2:
                    dve.wait_ge(fst_done[i % 2], 48 * (i // 2))
                v.tensor_scalar(dtc[:, i % 2], spl[:, i].rearrange("p k m -> p (k m)"), DT_R / SHARP, DT_C, ALU.mult, ALU.add)\
                    .then_inc(dt_ready, 1)
                dve.wait_ge(dt_ready, i + 1)
                if i >= 2:
                    dve.wait_ge(sq_ready, i - 1)
                v.tensor_tensor(dxc[:, i % 2].rearrange("p (t b k) -> p k b t", b=NB, k=DH),
                                dtc[:, i % 2].rearrange("p (k b t) -> p k b t", k=DH, b=NB), xnT[:, i], ALU.mult).then_inc(fst_ready, 1)
                if i >= 1:
                    norm_of_input(i - 1)
                v.tensor_tensor(sqb, be[:, i * P:(i + 1) * P, 0], be[:, i * P:(i + 1) * P, 0], ALU.mult).then_inc(sqb_ready, 1)
            norm_of_input(CH - 1)
            dve.wait_ge(e_used, CH)
            dve.wait_ge(route_ready, 1)
            dve.sem_inc(loop_go, 1)
            dve.wait_ge(loop_go, 5)

            for s_, c_ in ((T_ready, BLK), (v_ready, BLK), (ac_ready, BLK), (m_ready, BLK), (h_ready, BLK), (q_ready, BLK)):
                dve.sem_inc(s_, c_)
            v.memset(hr, 0.0).then_inc(h_ready, 1)
            v.memset(qv, 1.0).then_inc(q_ready, 1)
            svb = lambda slot: sv[:, slot, :].unsqueeze(2).broadcast_to([P, 2, 32])
            tr2 = tr.rearrange("p (w c) -> p w c", w=2)
            dve.wait_ge(s_ready, BLK)
            dve.wait_ge(u_done, 2)
            with dve.Fori(0, NT // RING) as r:
                for k in range(RING):
                    before = (k - 1) % RING
                    now = r * RING + (k + 1 + BLK)
                    dve.wait_ge(h_ready, now)
                    v.tensor_tensor(vv, hr[:, before, :], da[:, k, :], ALU.mult).then_inc(v_ready, 1)
                    dve.wait_ge(q_ready, now)
                    v.tensor_scalar(mx, qv, 1.0, None, ALU.max).then_inc(m_ready, 1)
                    dve.wait_ge(v_ready, now)
                    v.tensor_tensor_reduce(out=junk[:, 0, :], in0=vv, in1=ur[:, k, :], scale=2.0, scalar=0.0,
                                           op0=ALU.mult, op1=ALU.add, accum_out=ac[:, 1:2])
                    if k % QUAD == QUAD - 1:
                        dve.wait_ge(u_done, r * (RING // QUAD) + (k // QUAD + 3))
                    elif k % BLK == 0:
                        dve.wait_ge(y_done, r * 2 + (k // BLK + 2))
                    v.tensor_tensor_reduce(out=junk[:, 1, :], in0=vv, in1=vv, scale=1.0, scalar=0.0,
                                           op0=ALU.mult, op1=ALU.add, accum_out=ac[:, 0:1]).then_inc(ac_ready, 1)
                    dve.wait_ge(m_ready, now)
                    v.reciprocal(sv[:, before, 0:1], mx)
                    dve.wait_ge(ac_ready, now)
                    v.transpose(tr, ac.unsqueeze(2).broadcast_to([P, 2, 32])).then_inc(T_ready, 1)
                    dve.wait_ge(s_ready, now)
                    v.scalar_tensor_tensor(hr[:, k, :], vv, sv[:, before, 1:2], ur[:, k, :], ALU.mult, ALU.add)\
                        .then_inc(h_ready, 1)
                    dve.wait_ge(T_ready, now)
                    v.tensor_tensor_reduce(out=junkq.rearrange("p (w c) -> p w c", w=2), in0=tr2, in1=svb(before),
                                           scale=1.0 / CLAMP ** 2, scalar=ring_be[:, k, 1:2],
                                           op0=ALU.mult, op1=ALU.add, accum_out=qv).then_inc(q_ready, 1)
            dve.wait_ge(q_ready, NT + 1 + BLK)
            v.tensor_scalar(mx, qv, 1.0, None, ALU.max).then_inc(m_ready, 1)

            def last_product(i):
                f = i % 2
                dve.wait_ge(silu_done, i + 1)
                dve.wait_ge(fin_x[f], 16 * (i // 2 + 1))
                dve.wait_ge(fin_y[f], 16 * (i // 2 + 1))
                v.tensor_tensor(sl[:, f], sl[:, f], yl[:, f], ALU.mult).then_inc(f_mul, 1)
                dve.wait_ge(f_mul, i + 1)
                if i >= 2:
                    dve.wait_ge(o_out[f], 16 * (i // 2))
                v.tensor_tensor(ol[:, f], sl[:, f], xl[:, f], ALU.add).then_inc(o_ready, 1)

            for i in range(CH):
                f = i % 2
                dve.wait_ge(fin_g[f], 16 * 2 * NB * (i // 2 + 1))
                if i >= 2:
                    dve.wait_ge(silu_done, i - 1)
                for b in range(NB):
                    v.tensor_scalar(fm[:, f, b, :], g0[:, f, b, :], wsel[:, 0, b * CH + i:b * CH + i + 1], None,
                                    ALU.mult).then_inc(f_half, 1)
                for b in range(NB):
                    dve.wait_ge(f_half, NB * i + b + 1)
                    v.scalar_tensor_tensor(fm[:, f, b, :], g1[:, f, b, :], wsel[:, 1, b * CH + i:b * CH + i + 1],
                                           fm[:, f, b, :], ALU.mult, ALU.add).then_inc(f_ready, 1)
                if i >= 1:
                    last_product(i - 1)
            last_product(CH - 1)


        @block.scalar
        def _(act):
            a = nc.scalar
            links = [0]

            def link(ins):
                links[0] += 1
                ins.then_inc(act_chain, 1)
                act.wait_ge(act_chain, links[0])

            act.wait_ge(ld_v, 48)
            act.wait_ge(consts, CONSTS)
            a.activation(alog, alog, ACT.Tanh, scale=0.1).then_inc(a_tanh, 1)
            act.wait_ge(a_tanh, 1)
            a.activation(alog, alog, ACT.Exp, scale=10.0).then_inc(a_exp, 1)
            a.preload_act_table_set("natural_log_exp_and_others")
            def turned(i):
                act.wait_ge(xt_ps, i + 1)
                for k in range(DH):
                    last = a.activation(xnT[:, i, k].rearrange("p b t -> p (b t)"), ps[TURN_BANKS[i % 2][k]][:, :], ACT.Copy)
                last.then_inc(xt_sb, 1)

            turned(0)
            for i in range(CH):
                if i + 1 < CH:
                    turned(i + 1)
                act.wait_ge(z_ps, i + 1)
                if i >= 2:
                    act.wait_ge(sp_ready, i - 1)
                for k in range(DH):
                    a.activation(rel[:, i % 2, k, :], ps[2 + k][:, :], ACT.Relu, bias=bdt_sb[:, k:k + 1])
                    last = a.activation(spl[:, i, k, :], ps[2 + k][:, :], ACT.Abs, bias=bdt_sb[:, k:k + 1])
                last.then_inc(z_used, 1)
                act.wait_ge(z_used, i + 1)
                link(a.activation(spl[:, i], spl[:, i], ACT.Exp, scale=-1.0))
                a.activation(spl[:, i], spl[:, i], ACT.Ln, bias=1.0).then_inc(sp_half, 1)

            def soft_clamp(i):
                act.wait_ge(sp_ready, i + 1)
                a.activation(spl[:, i], spl[:, i], ACT.Tanh, bias=dtbias[:, :], scale=SHARP / (DT_R + 1e-8)).then_inc(th_ready, 1)

            soft_clamp(0)
            soft_clamp(1)
            for i in range(CH):
                if i + 2 < CH:
                    soft_clamp(i + 2)
                if i == 0:
                    act.wait_ge(gap_ready, 1)
                    a.activation(pw[:, 3, :], pw[:, 0, :], ACT.Exp).then_inc(gap_exp, 1)
                act.wait_ge(fst_ready, i + 1)
                if i >= 1:
                    act.wait_ge(e_ps, i)
                a.activation(sq.rearrange("p k (b t) -> p k b t", b=NB), dxc[:, i % 2].rearrange("p (t b k) -> p k b t", b=NB, k=DH),
                             ACT.Square).then_inc(sq_ready, 1)
            act.wait_ge(sq_ready, CH)
            act.sem_inc(loop_go, 1)
            act.wait_ge(loop_go, 5)
            act.sem_inc(da_done, 2)
            act.sem_inc(u_done, 1)
            act.sem_inc(gelu_done, 2)
            act.sem_inc(ye_sb, 1)

            def tanh_ops(f, first, count):
                src = stage[:, f, 0, :].rearrange("p (k b t) -> p b k t", b=NB, k=DH)
                dst = tanhb[:, f, :, :].rearrange("p (b k n) t -> p b k n t", b=NB, k=DH)
                for c in range(first, first + count):
                    k, n_ = divmod(c, NS)
                    last = a.activation(dst[:, :, k, n_, :], src[:, :, k, :], ACT.Tanh, scale=a16[:, c:c + 1])
                return last

            def decay_ops(f):
                for c in range(4):
                    flat = tanhb[:, f, c * 32:(c + 1) * 32, :].rearrange("p s t -> p (s t)")
                    last = a.activation(flat, flat, ACT.Exp, scale=16.0)
                return last

            act.wait_ge(a_ready, 1)
            act.wait_ge(stage_in, 16)
            tanh_ops(0, 0, DH * NS).then_inc(tanh_done, 1)
            act.wait_ge(tanh_done, 1)
            decay_ops(0).then_inc(decay_ready, 1)
            act.wait_ge(xt_tp, 1)
            a.activation(xt.rearrange("p k s -> p (k s)"), ps[6][:, :], ACT.Copy).then_inc(xt_in, 1)

            def inputs_out_of_psum(n):
                act.wait_ge(x_ps, n + 1)
                a.activation(xin, ps[3][:, P:2 * P], ACT.Copy).then_inc(x_sb, 1)

            inputs_out_of_psum(0)

            def y_out_of_psum(n):
                act.wait_ge(y_done, n + 2)
                act.wait_ge(y_out, n * 16 + 1)
                a.activation(ysb, ps[3][:, 0:P], ACT.Copy).then_inc(y_sb, 1)

            with act.Fori(0, CH) as m:
                for g in range(BPB):
                    half, f = g % 2, g // 4
                    act.wait_ge(q_ready, m * P + (g * BLK + 1))
                    a.activation(ring_be[:, half * BLK:(half + 1) * BLK, :], be[:, bass.ds(m * P + g * BLK, BLK), :],
                                 ACT.Copy).then_inc(be_stage, 1)
                    for q in range(QPB):
                        t = half * BLK + q * QUAD
                        quads = m * (P // QUAD) + (g * QPB + q)
                        act.wait_ge(ta_ps, quads + 2)
                        a.activation(da[:, t:t + QUAD, :].rearrange("p t d -> p (t d)"), ps[q % 2][:, :], ACT.Copy)\
                            .then_inc(da_done, 1)
                        if q == 0:
                            act.wait_ge(be_stage, m * BPB + (g + 1))
                        act.wait_ge(tu_ps, quads + 1)
                        for j in range(QUAD):
                            last = a.activation(ur[:, t + j, :], ps[2][:, j * P:(j + 1) * P], ACT.Copy,
                                                scale=ring_be[:, t + j, 0:1])
                        last.then_inc(u_done, 1)
                        if q == 1:
                            y_out_of_psum(m * BPB + g)
                        for kind, i, j, _ in by_quad[g * QPB + q]:
                            if kind == "up":
                                if j == 0:
                                    act.wait_ge(mm2_ps, m * (TPE * 2) + (i * 2 + 1))
                                act.wait_ge(mm1_ps, m * (TPE * FC // 2) + (i * FC // 2 + j + 2))
                                a.activation(hid[:, 2 * j:2 * j + 2, :].rearrange("p c s -> p (c s)"), ps[4 + j % 2][:, :],
                                             ACT.Gelu).then_inc(gelu_done, 1)
                            elif kind == "turn":
                                act.wait_ge(xt_tp, m * TPE + (i + 2))
                                a.activation(xt.rearrange("p k s -> p (k s)"), ps[6][:, :], ACT.Copy).then_inc(xt_in, 1)
                            elif j == 1:
                                act.wait_ge(mm2_ps, m * (TPE * 2) + (i * 2 + 3))
                                act.wait_ge(ye_out, m * (16 * TPE) + (i * 16 + 1))
                                a.activation(yrow.rearrange("p c d -> p (c d)"), ps[7][:, :], ACT.Copy).then_inc(ye_sb, 1)
                        if q == QPB - 1:
                            inputs_out_of_psum(m * BPB + (g + 1))
                        if g % 4 == 0 and q == 0:
                            act.wait_ge(stage_in, m * 32 + (16 * (f + 2)))
                            act.wait_ge(ta_ps, m * (P // QUAD) + (f * (HALF // QUAD) + 1))
                        last = tanh_ops(1 - f, 2 * (QPB * (g % 4) + q), 2)
                    if g % 4 == 3:
                        last.then_inc(tanh_done, 1)
                        act.wait_ge(tanh_done, m * 2 + (f + 2))
                        decay_ops(1 - f).then_inc(decay_ready, 1)
            act.sem_inc(u_done, 1)
            for n in range(NBLK, NBLK + 2):
                y_out_of_psum(n)
            for i in range(CH):
                act.wait_ge(f_ready, NB * (i + 1))
                if i >= 2:
                    act.wait_ge(o_ready, i - 1)
                a.activation(sl[:, i % 2], fm[:, i % 2], ACT.Silu).then_inc(silu_done, 1)

        @block.tensor
        def _(pe):
            t = nc.tensor
            pe.wait_ge(consts, CONSTS)
            pe.wait_ge(ld_w, 64)
            def turn(i):
                pe.wait_ge(xn_ready, i + 1)
                if i >= 2:
                    pe.wait_ge(xt_sb, i - 1)
                for k in range(DH):
                    for b in range(NB):
                        last = t.transpose(ps[TURN_BANKS[i % 2][k]][:, b * P:(b + 1) * P], xnat[:, b, i, k * P:(k + 1) * P], ident[:, :])
                last.then_inc(xt_ps, 1)

            turn(0)
            for i in range(CH):
                if i + 1 < CH:
                    turn(i + 1)
                pe.wait_ge(xt_sb, i + 1)
                if i >= 1:
                    pe.wait_ge(z_used, i)
                for h in range(DH):
                    for k in range(DH):
                        last = t.matmul(ps[2 + h][:, :], wdt_sb[:, k, h * P:(h + 1) * P],
                                        xnT[:, i, k].rearrange("p b t -> p (b t)"), start=k == 0, stop=k == DH - 1)
                last.then_inc(z_ps, 1)
                if i >= 1:
                    pe.wait_ge(bc_sb, i)
                for w, sbw in enumerate((wb_sb, wc_sb)):
                    for b in range(NB):
                        for k in range(DH):
                            last = t.matmul(ps[4][32 * b:32 * b + 32, w * P:(w + 1) * P], sbw[:, k, :], xnT[:, i, k, b, :],
                                            start=k == 0, stop=k == DH - 1)
                last.then_inc(bc_ps, 1)
                for b in range(NB):
                    j = b * CH + i
                    for k in range(DH):
                        last = t.matmul(ps[6][:, j * NE:(j + 1) * NE], xnT[:, i, k, b, :], wg_sb[:, k, :],
                                        start=k == 0, stop=k == DH - 1)
                if i == CH - 1:
                    last.then_inc(lg_ps, 1)
            pe.wait_ge(rt_in, 1)
            flat = ohb.rearrange("p e k j -> p (e k j)")
            t.matmul(ps[7][:, :], lows, flat, start=True, stop=True)
            t.matmul(ps[6][:, :], ones[:, :], flat, start=True, stop=True).then_inc(rank_ps, 1)
            for i in range(CH):
                pe.wait_ge(sq_ready, i + 1)
                if i >= 1:
                    pe.wait_ge(e_used, i)
                for b in range(NB):
                    for k in range(DH):
                        t.matmul(ps[5][32 * b:32 * b + 32, 0:P], ones[:, 0:32], sq[:, k, b * P:(b + 1) * P],
                                 start=k == 0, stop=k == DH - 1)
                pe.wait_ge(sqb_ready, i + 1)
                t.matmul(ps[5][:, P:2 * P], bsum[:, :], sqb, start=True, stop=True).then_inc(e_ps, 1)
            pe.wait_ge(e_ps, CH)
            pe.sem_inc(loop_go, 1)
            pe.wait_ge(loop_go, 5)
            pe.sem_inc(mm1_ps, 1)
            pe.sem_inc(mm2_ps, 1)
            pe.sem_inc(y_done, 1)
            pe.sem_inc(ta_ps, 1)

            def turn_rows(n):
                for k in range(DH):
                    for c in range(2):
                        last = t.transpose(ps[6][:, k * TS + c * P:k * TS + (c + 1) * P], xrow[:, c, k * P:(k + 1) * P], ident[:, :])
                return last

            pe.wait_ge(xrow_in, 16)
            turn_rows(0).then_inc(xt_tp, 1)

            def turn_inputs(f, block_):
                c = block_ * P
                return t.transpose(ps[3][:, P:2 * P], stage[:, f, 1, c:c + P], ident[:, :])

            pe.wait_ge(stage_in, 16)
            turn_inputs(0, 0).then_inc(x_ps, 1)

            def output(n, count, half):
                pe.wait_ge(win_ready, n + 1)
                pe.wait_ge(h_ready, count)
                pe.wait_ge(dx_in, (n + 1) * 16)
                t.matmul(ps[3][:, 0:P], ident[:, :], dxt, start=True, stop=False)
                for j in range(BLK):
                    last = t.matmul(ps[3][:, 0:P], win[:, j, BLK - 1 - j:2 * BLK - 1 - j, :].rearrange("p c g -> p (c g)"), hr[:, half * BLK + j, :],
                                    start=False, stop=j == BLK - 1)
                last.then_inc(y_done, 1)

            pe.wait_ge(h_ready, BLK + 1)
            with pe.Fori(0, CH) as m:
                for g in range(BPB):
                    f = g // 4
                    if g % 4 == 0:
                        pe.wait_ge(decay_ready, m * 2 + (f + 1))
                    pe.wait_ge(x_sb, m * BPB + (g + 1))
                    for q in range(QPB):
                        quads = m * (P // QUAD) + (g * QPB + q)
                        pe.wait_ge(da_done, quads + 1)
                        for j in range(QUAD):
                            s = (g % 4) * BLK + q * QUAD + j
                            last = t.transpose(ps[q % 2][:, j * P:(j + 1) * P], tanhb[:, f, :, s], ident[:, :])
                        last.then_inc(ta_ps, 1)
                        pe.wait_ge(u_done, quads + 1)
                        for j in range(QUAD):
                            last = t.matmul(ps[2][:, j * P:(j + 1) * P], pick[:, q * QUAD + j, :], xin, start=True, stop=True)
                        last.then_inc(tu_ps, 1)
                        if q == 1:
                            output(m * BPB + g, m * P + (g * BLK + 1), g % 2)
                        for kind, i, j, _ in by_quad[g * QPB + q]:
                            if kind == "up":
                                if j == 0:
                                    if i == 0:
                                        pe.wait_ge(wf_in, m * 16 + 16)
                                    pe.wait_ge(xt_in, m * TPE + (i + 1))
                                pe.wait_ge(gelu_done, m * (TPE * FC // 2) + (i * FC // 2 + j + 1))
                                for c in range(2):
                                    for k in range(DH):
                                        last = t.matmul(ps[4 + j % 2][:, c * TS:(c + 1) * TS],
                                                        wf[:, k, (2 * j + c) * P:(2 * j + c + 1) * P], xt[:, k, :],
                                                        start=k == 0, stop=k == DH - 1)
                                last.then_inc(mm1_ps, 1)
                            elif kind == "turn":
                                pe.wait_ge(xrow_in, m * (16 * TPE) + 16 * (i + 2))
                                turn_rows(i + 1).then_inc(xt_tp, 1)
                            else:
                                if j == 0:
                                    if i == 0:
                                        pe.wait_ge(wp_in, m * 16 + 16)
                                    pe.wait_ge(gelu_done, m * (TPE * FC // 2) + ((i + 1) * FC // 2 + 2))
                                    pe.wait_ge(ye_sb, m * TPE + (i + 1))
                                for k in range(FC):
                                    last = t.matmul(ps[7][:, j * D:(j + 1) * D], hid[:, k, j * P:(j + 1) * P], wp[:, k, :],
                                                    start=k == 0, stop=k == FC - 1)
                                last.then_inc(mm2_ps, 1)
                    pe.wait_ge(y_sb, m * BPB + (g + 1))
                    if g % 4 == 3:
                        pe.wait_ge(stage_in, m * 32 + 16 * (f + 2))
                    turn_inputs((g + 1) // 4 % 2, (g + 1) % 4).then_inc(x_ps, 1)
            pe.wait_ge(x_sb, NBLK + 1)
            for n in range(NBLK, NBLK + 2):
                if n > NBLK:
                    pe.wait_ge(y_sb, n)
                output(n, (n - 1) * BLK + BLK + 1, n % 2)


def kernel(**inputs):
    import numpy as _np
    import concourse.bacc as _bacc
    from concourse import mybir as _mybir
    from concourse.bass_utils import run_bass_kernel_spmd as _run

    def state_columns(w):
        wt = _np.transpose(w)
        return _np.ascontiguousarray(_np.concatenate([wt] * DH, axis=1))

    laid = {
        "x": inputs["L0_attn_x"],
        "wdtT": _np.ascontiguousarray(_np.transpose(inputs["L0_attn_Wdt"])),
        "bdt": inputs["L0_attn_bdt"],
        "wb": state_columns(inputs["L0_attn_WB"]),
        "wc": state_columns(inputs["L0_attn_WC"]),
        "a_log": inputs["L0_attn_A_log"],
        "dpar": inputs["L0_attn_Dp"],
        "w_g": inputs["L0_ffn_w_g"],
        "c_fc": inputs["L0_ffn_c_fc"],
        "c_proj": inputs["L0_ffn_c_proj"],
    }
    nc = _bacc.Bacc("TRN2", target_bir_lowering=False, num_devices=1)
    arrays, args = {}, []
    for name, a in laid.items():
        a = _np.ascontiguousarray(a)
        arrays[f"in_{name}"] = a
        args.append(nc.dram_tensor(f"in_{name}", a.shape, _mybir.dt.from_np(a.dtype), kind="ExternalInput").ap())
    out = nc.dram_tensor("out_0", (NB, NT, D), _mybir.dt.float32, kind="ExternalOutput").ap()
    build(nc, *args, out)
    r = _run(nc, [arrays], core_ids=[0])
    return r.results[0]["out_0"]
```

```python
from contextlib import ExitStack

import concourse.bass as bass
from concourse import mybir

NB, NT, D, NS = 4, 1024, 256, 16
NE, CAP, FF = 8, 1280, 1024
P = 128
DH = D // P
TOK = NB * NT
TILES = TOK // P
CH = NT // P
HALF = 64
NHALF = NT // HALF
BLK = 16
NBLK = NT // BLK
BPB = P // BLK
QUAD = 4
QPB = BLK // QUAD
RING = 2 * BLK
SLOTS = NE * CAP
TS = 256
TPE = CAP // TS
SC = SLOTS // P
EC = CAP // P
YPAD = 2 * BLK
FC = FF // P
CLAMP = 20.0
DT_LO, DT_HI, SHARP = 0.001, 0.1, 0.5
DT_C, DT_R = (DT_HI + DT_LO) / 2, (DT_HI - DT_LO) / 2
WIN = 2 * BLK - 1
NG = NB * DH
BC_BANKS = (4, 0)
Z_BANKS = ((2, 3), (5, 7))
CONSTS = 22


def build(nc, x, wdtT, bdt, wb, wc, a_log, dpar, w_g, c_fc, c_proj, out):
    f32, i32 = mybir.dt.float32, mybir.dt.int32
    ALU, ACT, AX = mybir.AluOpType, mybir.ActivationFunctionType, mybir.AxisListType
    ctx = ExitStack()
    with ctx:
        def sb(name, shape, dt=f32):
            return ctx.enter_context(nc.sbuf_tensor(name, shape, dt))

        def sem(name):
            return ctx.enter_context(nc.semaphore(name))

        xnd = nc.dram_tensor("xnd", (TOK + P, D), f32, kind="Internal").ap()
        moe = nc.dram_tensor("moe", (2 * TOK + P, D), f32, kind="Internal").ap()
        feed = nc.dram_tensor("feed", (CH + 1, P, 2, NB * DH * P), f32, kind="Internal").ap()
        dx = nc.dram_tensor("dx", (NT + YPAD, NB, D), f32, kind="Internal").ap()
        ys = nc.dram_tensor("ys", (NT + YPAD, NB, D), f32, kind="Internal").ap()

        ident = sb("ident", [P, P])
        ones = sb("ones", [P, P])
        bsum = sb("bsum", [P, P])
        winmask = sb("winmask", [P, 8])
        zeros = sb("zeros", [P, 2 * D])
        neghalf = sb("neghalf", [P, NB])
        pick = sb("pick", [P, BLK, P])
        xrow = sb("xrow", [P, 2, D])
        dtbias = sb("dtbias", [P, 1])
        a16 = sb("a16", [P, DH * NS])
        be = sb("be", [P, NT, 2])
        ccol = sb("ccol", [P, BLK + NT])
        mv = sb("mv", [P, TILES, 2])
        rstd = sb("rstd", [P, TILES])
        wsel = sb("wsel", [P, 2, TILES])
        slot_src = sb("slot_src", [P, SC + EC], i32)
        slot_dst = sb("slot_dst", [P, SC], i32)
        src_now = sb("src_now", [P, EC], i32)
        dst_now = sb("dst_now", [P, EC], i32)

        ARENA = 40704
        arena = sb("arena", [P, ARENA])
        at = [0]

        def take(n):
            at[0] += n
            assert at[0] <= ARENA, at[0]
            return arena[:, at[0] - n:at[0]]

        SD = NB * DH * HALF
        tanhb = take(2 * P * HALF).rearrange("p (f s t) -> p f s t", f=2, t=HALF)
        stage = take(2 * 2 * SD).rearrange("p (f w s) -> p f w s", f=2, w=2)
        da = take(RING * P).rearrange("p (t d) -> p t d", d=P)
        ur = take(RING * P).rearrange("p (t d) -> p t d", d=P)
        hr_at = at[0]
        hr = take(RING * P).rearrange("p (t d) -> p t d", d=P)
        win = take(BLK * NG * WIN).rearrange("p (t c g) -> p t c g", g=NG, c=WIN)
        xt = take(DH * TS).rearrange("p (k s) -> p k s", k=DH)
        hid = take(FC * TS).rearrange("p (k s) -> p k s", k=FC)
        yrow = take(2 * D).rearrange("p (c d) -> p c d", c=2)
        wf = sb("wf", [P, DH, FF])[:, :, :]
        wp = sb("wp", [P, FC, D])[:, :, :]
        ysb = take(P)
        xin = take(P)
        dxt = take(P)
        vv = take(P)
        junk = take(2 * P).rearrange("p (f d) -> p f d", f=2)
        junkq = take(64)
        ac = take(2)
        tr = take(64)
        qv = take(1)
        mx = take(1)
        sv = take(RING * 2).rearrange("p (t w) -> p t w", w=2)
        cs = take(BLK)
        ring_be = take(RING * 2).rearrange("p (t w) -> p t w", w=2)

        at2 = [0]

        def lay(n):
            at2[0] += n
            assert at2[0] <= ARENA, at2[0]
            return arena[:, at2[0] - n:at2[0]]

        xnat = lay(TILES * D).rearrange("p (b i d) -> p b i d", b=NB, i=CH)
        xnT = lay(CH * DH * NB * P).rearrange("p (i k b t) -> p i k b t", i=CH, k=DH, b=NB)
        spl = lay(CH * DH * NB * P).rearrange("p (i k m) -> p i k m", i=CH, k=DH)
        rel = lay(2 * DH * NB * P).rearrange("p (f k m) -> p f k m", f=2, k=DH)
        fst = lay(2 * 2 * 2 * SD).rearrange("p (f w s) -> p f w s", f=2, w=2)
        dtc = fst[:, :, 0, :]
        dxc = fst[:, :, 1, :]
        sq = rel[:, 0]
        sqb = lay(P)
        dsb = lay(P)
        dxn = lay(2 * NB * D).rearrange("p (f b d) -> p f b d", f=2, b=NB)
        wdt_sb = lay(DH * D).rearrange("p (k m) -> p k m", k=DH)
        wb_sb = lay(DH * 32).rearrange("p (k m) -> p k m", k=DH)
        wc_sb = lay(DH * 32).rearrange("p (k m) -> p k m", k=DH)
        wg_sb = lay(DH * NE).rearrange("p (k m) -> p k m", k=DH)
        dpb = lay(D)
        bdt_sb = lay(DH)
        stats = lay(2 * NB * 6).rearrange("p (f b s) -> p f b s", f=2, b=NB)
        vare = lay(CH * NB).rearrange("p (i b) -> p i b", i=CH)
        JT = TILES
        lg = lay(NE * JT).rearrange("p (e j) -> p e j", e=NE)
        lgw = lay(NE * JT).rearrange("p (e j) -> p e j", e=NE)
        iom = lay(NE * JT).rearrange("p (e j) -> p e j", e=NE)
        iom_i = lay(NE * JT).bitcast(i32).rearrange("p (e j) -> p e j", e=NE)
        tmp = lay(NE * JT).rearrange("p (e j) -> p e j", e=NE)
        ohb = lay(NE * 2 * JT).rearrange("p (e k j) -> p e k j", e=NE, k=2)
        ohf = lay(NE * 2 * JT).rearrange("p (e k j) -> p e k j", e=NE, k=2)
        tot = lay(NE * 2 * JT).rearrange("p (e k j) -> p e k j", e=NE, k=2)
        inc = lay(NE * 2 * JT).rearrange("p (e k j) -> p e k j", e=NE, k=2)
        keepm = lay(NE * 2 * JT).rearrange("p (e k j) -> p e k j", e=NE, k=2)
        lows = lay(P)
        top = lay(2 * JT).rearrange("p (k j) -> p k j", k=2)
        eix = lay(2 * JT).rearrange("p (k j) -> p k j", k=2)
        rank = lay(2 * JT).rearrange("p (k j) -> p k j", k=2)
        keep = lay(2 * JT).rearrange("p (k j) -> p k j", k=2)
        lo = lay(2 * JT).rearrange("p (k j) -> p k j", k=2)
        hi = lay(2 * JT).rearrange("p (k j) -> p k j", k=2)
        rank_i = lay(2 * JT).bitcast(i32).rearrange("p (k j) -> p k j", k=2)
        lo_i = lay(2 * JT).bitcast(i32).rearrange("p (k j) -> p k j", k=2)
        hi_i = lay(2 * JT).bitcast(i32).rearrange("p (k j) -> p k j", k=2)
        rowid = lay(2 * JT).rearrange("p (k j) -> p k j", k=2)
        rowid_i = lay(2 * JT).bitcast(i32).rearrange("p (k j) -> p k j", k=2)
        cols_i = lay(P).bitcast(i32)
        cols = lay(P)
        pcol = lay(1)
        acc = lay(SC)
        free = lay(SC)
        dt0 = lay(SD)
        lohot = wp.rearrange("p k d -> p (k d)").rearrange("p (f n c) -> p f n c", f=2, n=8)
        wflat = wf.rearrange("p k d -> p (k d)")
        hihot = wflat[:, 0:8 * SC].rearrange("p (n c) -> p n c", n=8)
        hirow = wflat[:, 8 * SC:24 * SC].rearrange("p (f n c) -> p f n c", f=2, n=8)
        pw = lay(4 * JT).rearrange("p (k j) -> p k j", k=4)
        alog = lay(DH * NS)

        at3 = [0]

        def end(n):
            at3[0] += n
            assert at3[0] <= ARENA, at3[0]
            return arena[:, at3[0] - n:at3[0]]

        def chunks(count):
            return end(count * NB * D).rearrange("p (i b d) -> p i b d", i=count, b=NB)

        xl, yl, g0 = chunks(CH), chunks(CH), chunks(CH)
        end(hr_at - at3[0])
        g1_late, fm, sl = chunks(CH // 2), chunks(2), chunks(2)
        w4 = "p k (i b d) -> p (k i) b d"
        wf4, wp4 = wf.rearrange(w4, i=1, b=NB), wp.rearrange("p (i b) d -> p i b d", b=NB)
        g1 = [wf4[:, 0], wf4[:, 1], wp4[:, 0], wp4[:, 1]] + [g1_late[:, i] for i in range(CH // 2)]

        ps = [ctx.enter_context(nc.psum_tensor(f"ps{i}", [P, 512], f32)) for i in range(8)]

        ld_x = [sem(f"ld_x{k}") for k in range(CH)]
        ld_w = sem("ld_w")
        ld_v = sem("ld_v")
        ld_d = sem("ld_d")
        memz = sem("memz")
        padz = sem("padz")
        moe_zero = sem("moe_zero")
        consts = sem("consts")
        stat_chain = sem("stat_chain")
        stat_ready = sem("stat_ready")
        rstd_ready = sem("rstd_ready")
        xn_ready = sem("xn_ready")
        xt_ps = sem("xt_ps")
        xt_sb = sem("xt_sb")
        z_ps = sem("z_ps")
        z_used = sem("z_used")
        act_chain = sem("act_chain")
        sp_half = sem("sp_half")
        sp_ready = sem("sp_ready")
        th_ready = sem("th_ready")
        bc_ps = sem("bc_ps")
        bc_sb = sem("bc_sb")
        sq_ready = sem("sq_ready")
        sqb_ready = sem("sqb_ready")
        e_ps = sem("e_ps")
        e_chain = sem("e_chain")
        e_used = sem("e_used")
        dt_ready = sem("dt_ready")
        fst_ready = sem("fst_ready")
        fst_done = [sem(f"fst_done{k}") for k in range(2)]
        dxn_ready = sem("dxn_ready")
        dx_done = [sem(f"dx_done{k}") for k in range(2)]
        lg_ps = sem("lg_ps")
        rt_in = sem("rt_in")
        rank_ps = sem("rank_ps")
        rt_chain = sem("rt_chain")
        gap_ready = sem("gap_ready")
        gap_exp = sem("gap_exp")
        route_ready = sem("route_ready")
        a_tanh = sem("a_tanh")
        a_exp = sem("a_exp")
        a_ready = sem("a_ready")
        xn_out = sem("xn_out")
        lo_ready = sem("lo_ready")
        hi_half = sem("hi_half")
        hi_ready = sem("hi_ready")
        hot_used = sem("hot_used")
        slots_ready = sem("slots_ready")
        dt0_ready = sem("dt0_ready")
        rows_staged = sem("rows_staged")
        loop_go = sem("loop_go")
        init_win = sem("init_win")
        T_ready = sem("T_ready")
        h_ready = sem("h_ready")
        q_ready = sem("q_ready")
        v_ready = sem("v_ready")
        m_ready = sem("m_ready")
        s_ready = sem("s_ready")
        ac_ready = sem("ac_ready")
        ta_ps = sem("ta_ps")
        da_done = sem("da_done")
        tu_ps = sem("tu_ps")
        u_done = sem("u_done")
        be_stage = sem("be_stage")
        tanh_done = sem("tanh_done")
        stage_in = sem("stage_in")
        cs_ready = sem("cs_ready")
        win_ready = sem("win_ready")
        y_done = sem("y_done")
        y_sb = sem("y_sb")
        x_ps = sem("x_ps")
        x_sb = sem("x_sb")
        decay_ready = sem("decay_ready")
        y_out = sem("y_out")
        dx_in = sem("dx_in")
        xrow_in = sem("xrow_in")
        xt_tp = sem("xt_tp")
        xt_in = sem("xt_in")
        mm1_ps = sem("mm1_ps")
        gelu_done = sem("gelu_done")
        mm2_ps = sem("mm2_ps")
        ye_sb = sem("ye_sb")
        ye_out = sem("ye_out")
        yrow_free = sem("yrow_free")
        wf_in = sem("wf_in")
        wp_in = sem("wp_in")
        fin = [sem(f"fin{k}") for k in range(CH)]
        g_half = sem("g_half")
        f_ready = sem("f_ready")
        silu_done = sem("silu_done")
        f_mul = sem("f_mul")
        o_ready = sem("o_ready")
        o_out = sem("o_out")

        xn_tok = x.rearrange("b (i p) d -> p b i d", p=P)
        dx_tok = dx[YPAD:].rearrange("(i p) b d -> p i b d", p=P)
        ys_tok = ys[YPAD:].rearrange("(i p) b d -> p i b d", p=P)
        out_tok = out.rearrange("b (i p) d -> p b i d", p=P)

        work = [("turn", 0, 0, 1)]
        for i in range(TPE):
            work += [("up", i, j, 4) for j in range(FC // 2)]
            work += [("turn", i + 1, 0, 1)] if i + 1 < TPE else []
            work += [("down", i, c, 8) for c in range(2)]
        n = 6
        total = n + sum(w[3] for w in work)
        by_quad = [[] for _ in range(P // QUAD)]
        for w in work:
            by_quad[min(P // QUAD - 1, (n + w[3] // 2) * (P // QUAD) // total)].append(w)
            n += w[3]

        at_step = {}
        for qd, items in enumerate(by_quad):
            for kind, i, j, _ in items:
                if kind == "turn" or (kind == "down" and j == 1):
                    for c in range(2):
                        k = min(max(2, qd * QUAD - BLK + 3 * QUAD), P - 14) if c == 0 else k + (6 if kind == "down" else 1)
                        while k in at_step or k % BLK < 2:
                            k += 1
                        at_step[k] = (kind, i, c)
        freed_at = {k + 7: i for k, (kind, i, c) in at_step.items() if kind == "down" and c == 1}
        assert max(freed_at) < P, freed_at
        assert min(at_step) >= 0 and max(at_step) < P, at_step

        block = ctx.enter_context(nc.Block())

        @block.sync
        def _(sp):
            for i in range(CH):
                sp.dma_start(xnat[:, :, i, :], xn_tok[:, :, i, :]).then_inc(ld_x[i], 16)
                if i == 0:
                    sp.dma_start(wdt_sb, wdtT.rearrange("(k p) m -> p k m", p=P)).then_inc(ld_w, 16)
            sp.wait_ge(memz, 1)
            sp.dma_start(xnd[TOK:TOK + P, :], zeros[:, 0:D]).then_inc(padz, 16)
            for b in range(NB):
                sp.dma_start(dx[0:YPAD, b, :], zeros[0:YPAD, 0:D]).then_inc(padz, 16)
            for i in range(CH):
                sp.wait_ge(xn_ready, i + 1)
                sp.dma_start(xnd[0:TOK, :].rearrange("(b i p) d -> p b i d", p=P, i=CH)[:, :, i, :], xnat[:, :, i, :]).then_inc(xn_out, 16)
                sp.wait_ge(dxn_ready, i + 1)
                sp.dma_start(dx_tok[:, i], dxn[:, i % 2]).then_inc(dx_done[i % 2], 16)
                sp.dma_start(moe[i * NT:(i + 1) * NT, :].rearrange("(r p) d -> p r d", p=P),
                             zeros[:, 0:D].unsqueeze(1).broadcast_to([P, CH, D])).then_inc(moe_zero, 16)
            for i in range(CH):
                sp.wait_ge(fst_ready, i + 1)
                sp.dma_start(feed[i], fst[:, i % 2]).then_inc(fst_done[i % 2], 16)
            sp.dma_start(feed[CH], fst[:, 1]).then_inc(fst_done[0], 16)
            sp.wait_ge(fst_done[0], 16 * CH // 2 + 16)
            sp.wait_ge(fst_done[1], 16 * CH // 2)
            for k in range(2):
                sp.wait_ge(dx_done[k], 16 * CH // 2)
            sp.sem_inc(loop_go, 1)
            sp.wait_ge(padz, 16 * (NB + 1))
            sp.wait_ge(loop_go, 5)
            sp.sem_inc(y_out, 1)
            def load_feed(f, chunk):
                sp.dma_start(stage[:, f, 0, :].rearrange("p (g t) -> p g t", t=HALF),
                             feed[chunk, :, 0, :].rearrange("c p (g h t) -> (c p) h g t", h=2, t=HALF)[:, f]).then_inc(stage_in, 16)
                sp.dma_start(stage[:, f, 1, :],
                             feed[chunk, :, 1, :].rearrange("c p (h s) -> (c p) h s", h=2)[:, f]).then_inc(stage_in, 16)

            load_feed(0, slice(0, 1))
            sp.wait_ge(slots_ready, 1)
            sp.wait_ge(stage_in, 32)

            def load_dx(n, at):
                sp.wait_ge(y_done, n + 1)
                sp.dma_start(dxt, dx[at, :, :].rearrange("t b (k d) -> (t b k) d", k=DH)).then_inc(dx_in, 16)

            def store_y(n, at):
                sp.wait_ge(y_sb, n + 1)
                sp.dma_start(ys[at, :, :].rearrange("t b (k d) -> (t b k) d", k=DH), ysb).then_inc(y_out, 16)

            with sp.Fori(0, CH) as m:
                load_dx(m * BPB, bass.ds(m * P, BLK))
                sp.wait_ge(mm1_ps, m * (TPE * FC // 2) + 1)
                sp.dma_start(wf, c_fc[bass.ds(m, 1), :, :].rearrange("e (k p) f -> p (e k) f", p=P)).then_inc(wf_in, 16)
                sp.wait_ge(mm2_ps, m * (TPE * 2) + 1)
                sp.dma_start(wp, c_proj[bass.ds(m, 1), :, :].rearrange("e (k p) d -> p (e k) d", p=P)).then_inc(wp_in, 16)
                for g in range(BPB):
                    if g % 4 == 0:
                        f = g // 4
                        sp.wait_ge(tanh_done, m * 2 + f + 1)
                        load_feed(1 - f, bass.ds(m + f, 1))
                    if g > 0:
                        load_dx(m * BPB + g, bass.ds(m * P + g * BLK, BLK))
                    store_y(m * BPB + g, bass.ds(m * P + g * BLK, BLK))
            load_dx(NBLK, slice(NBLK * BLK, (NBLK + 1) * BLK))
            store_y(NBLK, slice(NBLK * BLK, (NBLK + 1) * BLK))
            load_dx(NBLK + 1, slice((NBLK + 1) * BLK, (NBLK + 2) * BLK))
            sp.wait_ge(decay_ready, NHALF + 1)
            for i in range(CH):
                if i >= 3:
                    sp.wait_ge(fin[i - 3], 16)
                sp.dma_start(xl[:, i], xn_tok[:, :, i, :]).then_inc(fin[i], 16)
            sp.wait_ge(ta_ps, NT // QUAD + 1)
            sp.wait_ge(y_out, 16 * (NBLK + 1) + 1)
            for i in range(CH - 1):
                sp.dma_start(yl[:, i], ys_tok[:, i]).then_inc(fin[i], 16)
            store_y(NBLK + 1, slice((NBLK + 1) * BLK, (NBLK + 2) * BLK))
            sp.wait_ge(ye_out, 32 * NE * TPE)
            sp.wait_ge(x_sb, NBLK + 1)
            for i in range(CH):
                for k, to in enumerate((g0[:, i], g1[i])):
                    sp.dma_start(to, moe[k * TOK:(k + 1) * TOK, :].rearrange("(b i p) d -> p b i d", p=P, i=CH)[:, :, i, :])\
                        .then_inc(fin[i], 16)
                if i == 0:
                    sp.wait_ge(y_out, 16 * (NBLK + 2) + 1)
                    sp.dma_start(yl[:, CH - 1], ys_tok[:, CH - 1]).then_inc(fin[CH - 1], 16)
            for i in range(CH):
                sp.wait_ge(o_ready, i + 1)
                sp.dma_start(out_tok[:, :, i, :], xl[:, i]).then_inc(o_out, 16)
            sp.wait_ge(o_out, 16 * CH)
            sp.wait_ge(xn_out, 16 * CH)

        @block.gpsimd
        def _(pool):
            g = nc.gpsimd
            n = [0]

            def made(ins):
                n[0] += 1
                ins.then_inc(consts, 1)

            g.memset(zeros[:, :], 0.0).then_inc(memz, 1)
            made(g.memset(ident[:, :], 0.0))
            made(g.memset(ones[:, :], 1.0))
            made(g.memset(pick[:, :, :], 0.0))
            made(g.memset(bsum[:, :], 0.5))
            made(g.memset(winmask[:, :], 1.0))
            made(g.memset(neghalf[:, :], -0.5))
            made(g.memset(dtbias[:, :], -DT_C * SHARP / (DT_R + 1e-8)))
            made(g.memset(lows, 1.0))
            made(g.memset(keepm, 1.0))
            made(g.memset(ccol[:, 0:BLK], 0.0))
            made(g.iota(iom_i, pattern=[[1, NE], [0, JT]], base=-NE, channel_multiplier=0))
            made(g.iota(rowid_i, pattern=[[TOK, 2], [P, JT]], base=-2 * TOK, channel_multiplier=1))
            made(g.iota(cols_i, pattern=[[1, P]], base=0, channel_multiplier=0))
            made(g.memset(slot_src[:, SC:], 0))
            pool.wait_ge(consts, n[0])
            made(g.affine_select(out=ident[:, :], in_=ident[:, :], compare_op=ALU.not_equal, fill=1.0, base=0,
                                 pattern=[[-1, P]], channel_multiplier=1))
            pk = pick[:, :, :].rearrange("p t (g n) -> p t g n", g=NG)
            made(g.affine_select(out=pk, in_=pk, compare_op=ALU.not_equal, fill=1.0, base=0,
                                 pattern=[[-NG, BLK], [-1, NG], [0, NS]], channel_multiplier=1))
            q4 = bsum[:, :].rearrange("p (b c) -> p b c", b=NB)
            made(g.affine_select(out=q4, in_=q4, compare_op=ALU.is_ge, fill=0.0, base=0,
                                 pattern=[[-32, NB], [0, 32]], channel_multiplier=1))
            made(g.affine_select(out=winmask[:, :], in_=winmask[:, :], compare_op=ALU.is_ge, fill=0.0, base=0,
                                 pattern=[[-NS, NG]], channel_multiplier=1))
            made(g.affine_select(out=lows, in_=lows, compare_op=ALU.is_gt, fill=0.0, base=0,
                                 pattern=[[1, P]], channel_multiplier=-1))
            made(g.memset(keepm[:, :, 0, 0:1], 0.0))
            pool.wait_ge(consts, n[0])
            made(g.affine_select(out=q4, in_=q4, compare_op=ALU.is_ge, fill=0.0, base=31,
                                 pattern=[[32, NB], [0, 32]], channel_multiplier=-1))
            made(g.affine_select(out=winmask[:, :], in_=winmask[:, :], compare_op=ALU.is_ge, fill=0.0, base=NS - 1,
                                 pattern=[[NS, NG]], channel_multiplier=-1))
            assert n[0] == CONSTS, n[0]
            rs = rstd[:, :].rearrange("p (b i) -> p b i", b=NB)
            for i in range(CH + 3):
                if i < CH:
                    pool.wait_ge(stat_ready, i + 1)
                    g.tensor_tensor(rs[:, :, i], vare[:, i, :], neghalf[:, :], ALU.pow).then_inc(rstd_ready, 1)
                if i >= 3:
                    c = i - 3
                    pool.wait_ge(sp_half, c + 1)
                    g.tensor_tensor(spl[:, c], spl[:, c], rel[:, c % 2], ALU.add).then_inc(sp_ready, 1)
            def time_steps(i):
                pool.wait_ge(th_ready, i + 1)
                if i >= 2:
                    pool.wait_ge(fst_done[i % 2], 16 * (i // 2))
                    pool.wait_ge(fst_ready, i - 1)
                g.tensor_scalar(dtc[:, i % 2], spl[:, i].rearrange("p k m -> p (k m)"), DT_R / SHARP, DT_C, ALU.mult, ALU.add)\
                    .then_inc(dt_ready, 1)

            def moe_rows(n):
                pool.wait_ge(hi_half, n + 1)
                if n >= 2:
                    pool.wait_ge(hot_used, n - 1)
                g.tensor_tensor(hirow[:, n % 2], hihot,
                                rowid.rearrange("p k j -> p (k j)")[:, 8 * n:8 * (n + 1)].unsqueeze(2).broadcast_to([P, 8, SC]),
                                ALU.mult).then_inc(hi_ready, 1)

            time_steps(0)
            g.tensor_scalar(dt0.rearrange("p (g t) -> p g t", t=HALF),
                            spl[:, 0].rearrange("p k (b h t) -> p h (k b) t", b=NB, h=2)[:, 0],
                            DT_R / SHARP, DT_C, ALU.mult, ALU.add).then_inc(dt0_ready, 1)
            for i in range(CH):
                if i + 1 < CH:
                    time_steps(i + 1)
                moe_rows(i)

            def gather(c, rows):
                g.indirect_dma_start(out=xrow[:, c, :], out_offset=None, in_=xnd,
                                     in_offset=bass.IndirectOffsetOnAxis(ap=rows, axis=0),
                                     bounds_check=TOK + P - 1, oob_is_err=True).then_inc(xrow_in, 16)

            def scatter(c, rows):
                g.indirect_dma_start(out=moe, out_offset=bass.IndirectOffsetOnAxis(ap=rows, axis=0),
                                     in_=yrow[:, c, :], in_offset=None,
                                     bounds_check=2 * TOK + P - 1, oob_is_err=True).then_inc(ye_out, 16)

            pool.sem_inc(loop_go, 1)
            pool.wait_ge(loop_go, 5)
            g.memset(win, 0.0).then_inc(init_win, 1)
            g.memset(sv, 1.0).then_inc(init_win, 1)
            pool.wait_ge(init_win, 2)
            pool.wait_ge(moe_zero, 16 * CH)
            pool.sem_inc(win_ready, 1)
            pool.sem_inc(s_ready, BLK)
            pool.wait_ge(xn_out, 16 * CH)
            pool.wait_ge(padz, 16 * (NB + 1))
            pool.wait_ge(slots_ready, 1)
            gather(0, slot_src[:, 0:1])
            gather(1, slot_src[:, 1:2])

            def scale_of(slot, count):
                pool.wait_ge(m_ready, count)
                g.tensor_tensor(sv[:, slot, 1:2], mx, neghalf[:, 0:1], ALU.pow).then_inc(s_ready, 1)

            def windows(half, ccols, count, blk):
                pool.wait_ge(s_ready, count)
                g.tensor_tensor(cs, ccols, sv[:, half * BLK:(half + 1) * BLK, 1], ALU.mult).then_inc(cs_ready, 1)
                pool.wait_ge(cs_ready, blk)
                pool.wait_ge(y_done, blk + 1)
                g.tensor_tensor(win[:, :, BLK - 1, :], cs.unsqueeze(2).broadcast_to([P, BLK, NG]),
                                winmask[:, :].unsqueeze(1).broadcast_to([P, BLK, NG]), ALU.mult).then_inc(win_ready, 1)

            with pool.Fori(0, CH) as m:
                for k in range(P):
                    if k in at_step:
                        kind, i, c = at_step[k]
                        if kind == "turn" and c == 0:
                            pool.wait_ge(xt_tp, m * TPE + (i + 1))
                        elif kind == "down" and c == 0:
                            pool.wait_ge(ye_sb, m * TPE + (i + 2))
                        elif kind == "down":
                            pool.wait_ge(ye_out, m * (32 * TPE) + (32 * i + 16))
                    if k in freed_at:
                        pool.wait_ge(ye_out, m * (32 * TPE) + 32 * (freed_at[k] + 1))
                    scale_of((k - 1) % RING, m * P + (k + 1 + BLK))
                    if k % BLK == 0:
                        windows(1 - k // BLK % 2, ccol[:, bass.ds(m * P + k, BLK)], m * P + (k + 1 + BLK), m * BPB + (k // BLK + 1))
                    if k == 1:
                        pool.wait_ge(xrow_in, m * (32 * TPE) + 32)
                        g.tensor_copy(src_now[:, :], slot_src[:, bass.ds(m * EC + 2, EC)]).then_inc(rows_staged, 1)
                        g.tensor_copy(dst_now[:, :], slot_dst[:, bass.ds(m * EC, EC)]).then_inc(rows_staged, 1)
                        pool.wait_ge(rows_staged, m * 2 + 2)
                    if k in freed_at:
                        pool.sem_inc(yrow_free, 1)
                    if k in at_step:
                        kind, i, c = at_step[k]
                        if kind == "turn":
                            gather(c, src_now[:, 2 * i + c:2 * i + c + 1])
                        else:
                            scatter(c, dst_now[:, 2 * i + c:2 * i + c + 1])
            scale_of(RING - 1, NT + 1 + BLK)
            windows(1, ccol[:, NT:NT + BLK], NT + 1 + BLK, NBLK + 1)
            for i in range(CH):
                pool.wait_ge(f_mul, i + 1)
                g.tensor_tensor(xl[:, i], sl[:, i % 2], xl[:, i], ALU.add).then_inc(o_ready, 1)

        @block.vector
        def _(dve):
            v = nc.vector

            links = [0]

            def link(ins):
                links[0] += 1
                ins.then_inc(stat_chain, 1)
                dve.wait_ge(stat_chain, links[0])

            mvt = mv[:, :, :].rearrange("p (b i) s -> p b i s", b=NB)

            def statistics(i):
                dve.wait_ge(ld_x[i], 16)
                for b in range(NB):
                    last = v.bn_stats(out=stats[:, i % 2, b, :], in_=xnat[:, b, i, :])
                link(last)
                for b in range(NB):
                    last = v.bn_aggr(out=mvt[:, b, i, :], in_=stats[:, i % 2, b, :])
                link(last)
                v.tensor_scalar(vare[:, i, :], mvt[:, :, i, 1], 1e-5, None, ALU.add).then_inc(stat_ready, 1)

            def normalize(i):
                dve.wait_ge(rstd_ready, i + 1)
                for b in range(NB):
                    j = b * CH + i
                    last = v.tensor_scalar(xnat[:, b, i, :], xnat[:, b, i, :], mv[:, j, 0:1], rstd[:, j:j + 1],
                                           ALU.subtract, ALU.mult)
                last.then_inc(xn_ready, 1)
                dve.wait_ge(xn_ready, i + 1)
                if i == 0:
                    dve.wait_ge(ld_d, 16)
                if i >= 2:
                    dve.wait_ge(dx_done[i % 2], 16 * (i // 2))
                v.tensor_tensor(dxn[:, i % 2, :, :], xnat[:, :, i, :], dpb.unsqueeze(1).broadcast_to([P, NB, D]),
                                ALU.mult).then_inc(dxn_ready, 1)

            statistics(0)
            for i in range(CH):
                if i + 1 < CH:
                    statistics(i + 1)
                normalize(i)
            dve.wait_ge(consts, CONSTS)
            dve.wait_ge(a_exp, 1)
            v.tensor_scalar(a16[:, :], alog, -1.0 / 16.0, None, ALU.mult).then_inc(a_ready, 1)
            hops = [0]

            def hop(ins):
                hops[0] += 1
                ins.then_inc(rt_chain, 1)
                dve.wait_ge(rt_chain, hops[0])

            dve.wait_ge(lg_ps, 1)
            hop(v.tensor_copy(iom, iom_i))
            hop(v.tensor_copy(rowid, rowid_i))
            hop(v.tensor_copy(cols, cols_i))
            hop(v.tensor_scalar(pcol, rowid[:, 0, 0:1], float(2 * TOK), None, ALU.add))
            hop(v.tensor_copy(lg, ps[6][:, 0:NE * JT].rearrange("p (j e) -> p e j", e=NE)))
            for k in range(2):
                cur = lg if k == 0 else lgw
                hop(v.tensor_reduce(out=top[:, k, :], in_=cur.rearrange("p e j -> p j e"), axis=AX.X, op=ALU.max))
                hop(v.tensor_tensor(tmp, cur, top[:, k, :].unsqueeze(1).broadcast_to([P, NE, JT]), ALU.is_equal))
                hop(v.tensor_tensor(tmp, tmp, iom, ALU.mult))
                hop(v.tensor_reduce(out=eix[:, k, :], in_=tmp.rearrange("p e j -> p j e"), axis=AX.X, op=ALU.min))
                hop(v.tensor_tensor(ohf[:, :, k, :], iom, eix[:, k, :].unsqueeze(1).broadcast_to([P, NE, JT]), ALU.is_equal))
                if k == 0:
                    hop(v.scalar_tensor_tensor(lgw, ohf[:, :, 0, :], -3e38, lg, ALU.mult, ALU.add))
            v.tensor_tensor(pw[:, 0, :], top[:, 1, :], top[:, 0, :], ALU.subtract).then_inc(gap_ready, 1)
            v.tensor_copy(ohb, ohf).then_inc(rt_in, 1)
            dve.wait_ge(gap_exp, 1)
            hop(v.tensor_scalar(pw[:, 1, :], pw[:, 3, :], 1.0, None, ALU.add))
            hop(v.reciprocal(pw[:, 2, :], pw[:, 1, :]))
            hop(v.tensor_tensor(pw[:, 3, :], pw[:, 3, :], pw[:, 2, :], ALU.mult))
            dve.wait_ge(rank_ps, 1)
            kj = "p e k j -> p (e k j)"
            hop(v.tensor_copy(tot, ps[6][:, :].rearrange("p (e k j) -> p e k j", e=NE, k=2)))
            hop(v.tensor_tensor_scan(inc.rearrange(kj), keepm.rearrange(kj), tot.rearrange(kj), 0.0, ALU.mult, ALU.add))
            hop(v.tensor_tensor(inc, inc, tot, ALU.subtract))
            hop(v.tensor_tensor(inc, inc, ps[7][:, :].rearrange("p (e k j) -> p e k j", e=NE, k=2), ALU.add))
            hop(v.tensor_tensor(inc, inc, ohf, ALU.mult))
            hop(v.tensor_reduce(out=rank, in_=inc.rearrange("p e k j -> p k j e"), axis=AX.X, op=ALU.add))
            hop(v.tensor_scalar(keep, rank, float(CAP), None, ALU.is_lt))
            hop(v.tensor_copy(rank_i, rank))
            v.tensor_scalar(lo_i, rank_i, P - 1, None, ALU.bitwise_and)
            hop(v.tensor_scalar(hi_i, rank_i, P.bit_length() - 1, None, ALU.logical_shift_right))
            v.tensor_copy(lo, lo_i)
            v.tensor_copy(hi, hi_i)
            hop(v.tensor_scalar(eix, eix, float(NE), float(EC), ALU.add, ALU.mult))
            hop(v.scalar_tensor_tensor(hi, hi, 1.0, eix, ALU.add, ALU.add))
            hop(v.tensor_tensor(hi, hi, keep, ALU.mult))
            v.tensor_scalar(hi, hi, -1.0, None, ALU.add).then_inc(rt_in, 1)
            v.tensor_tensor(wsel[:, :, :], pw[:, 2:4, :], keep, ALU.mult).then_inc(route_ready, 1)

            def one_hot(n):
                def each(a, c):
                    return a.rearrange("p k j -> p (k j)")[:, 8 * n:8 * (n + 1)].unsqueeze(2).broadcast_to([P, 8, c])

                if n >= 2:
                    dve.wait_ge(hot_used, n - 1)
                v.tensor_tensor(lohot[:, n % 2], cols.unsqueeze(1).broadcast_to([P, 8, P]), each(lo, P), ALU.is_equal)\
                    .then_inc(lo_ready, 1)
                if n >= 1:
                    dve.wait_ge(hi_ready, n)
                else:
                    dve.wait_ge(rt_in, 2)
                v.tensor_tensor(hihot, cols[:, 0:SC].unsqueeze(1).broadcast_to([P, 8, SC]), each(hi, SC), ALU.is_equal)\
                    .then_inc(hi_half, 1)

            def norm_of_input(i):
                cols = slice(i * P, (i + 1) * P)
                dve.wait_ge(e_ps, i + 1)
                v.tensor_copy(dsb, ps[5][:, P:2 * P]).then_inc(e_chain, 1)
                dve.wait_ge(e_chain, i + 1)
                v.scalar_tensor_tensor(be[:, cols, 1], ps[5][:, 0:P], 1.0 / CLAMP ** 2, dsb, ALU.mult, ALU.mult).then_inc(e_used, 1)

            dve.wait_ge(bc_sb, CH)
            for i in range(CH):
                dve.wait_ge(dt_ready, i + 1)
                if i >= 2:
                    dve.wait_ge(sq_ready, i - 1)
                    dve.wait_ge(fst_done[i % 2], 16 * (i // 2))
                v.tensor_tensor(dxc[:, i % 2].rearrange("p (t b k) -> p k b t", b=NB, k=DH),
                                dtc[:, i % 2].rearrange("p (k b t) -> p k b t", k=DH, b=NB), xnT[:, i], ALU.mult).then_inc(fst_ready, 1)
                if i >= 1:
                    norm_of_input(i - 1)
                v.tensor_tensor(sqb, be[:, i * P:(i + 1) * P, 0], be[:, i * P:(i + 1) * P, 0], ALU.mult).then_inc(sqb_ready, 1)
                one_hot(i)
            norm_of_input(CH - 1)
            dve.wait_ge(e_used, CH)
            dve.wait_ge(route_ready, 1)
            dve.sem_inc(loop_go, 1)
            dve.wait_ge(hot_used, CH)
            hop(v.tensor_scalar(acc, ps[7][:, 0:SC], float(2 * TOK), None, ALU.add))
            hop(v.tensor_scalar(free, acc, float(2 * TOK), pcol, ALU.is_equal, ALU.mult))
            hop(v.tensor_tensor(acc, acc, free, ALU.add))
            v.tensor_copy(slot_dst[:, :], acc)
            hop(v.tensor_scalar(free, acc, float(TOK), -float(TOK), ALU.is_ge, ALU.mult))
            hop(v.tensor_tensor(free, free, acc, ALU.add))
            v.tensor_copy(slot_src[:, 0:SC], free).then_inc(slots_ready, 1)
            dve.wait_ge(loop_go, 5)

            for s_, c_ in ((T_ready, BLK), (v_ready, BLK), (ac_ready, BLK), (m_ready, BLK), (h_ready, BLK), (q_ready, BLK)):
                dve.sem_inc(s_, c_)
            v.memset(hr, 0.0).then_inc(h_ready, 1)
            v.memset(qv, 1.0).then_inc(q_ready, 1)
            svb = lambda slot: sv[:, slot, :].unsqueeze(2).broadcast_to([P, 2, 32])
            tr2 = tr.rearrange("p (w c) -> p w c", w=2)
            dve.wait_ge(s_ready, BLK)
            dve.wait_ge(u_done, 2)
            with dve.Fori(0, CH) as m:
                for k in range(P):
                    slot, before = k % RING, (k - 1) % RING
                    now = m * P + (k + 1 + BLK)
                    dve.wait_ge(h_ready, now)
                    v.tensor_tensor(vv, hr[:, before, :], da[:, slot, :], ALU.mult).then_inc(v_ready, 1)
                    dve.wait_ge(q_ready, now)
                    v.tensor_scalar(mx, qv, 1.0, None, ALU.max).then_inc(m_ready, 1)
                    dve.wait_ge(v_ready, now)
                    v.tensor_tensor_reduce(out=junk[:, 0, :], in0=vv, in1=ur[:, slot, :], scale=2.0, scalar=0.0,
                                           op0=ALU.mult, op1=ALU.add, accum_out=ac[:, 1:2])
                    if k % QUAD == QUAD - 1:
                        dve.wait_ge(u_done, m * (P // QUAD) + (k // QUAD + 3))
                    elif k % BLK == 0:
                        dve.wait_ge(y_done, m * BPB + (k // BLK + 2))
                    v.tensor_tensor_reduce(out=junk[:, 1, :], in0=vv, in1=vv, scale=1.0, scalar=0.0,
                                           op0=ALU.mult, op1=ALU.add, accum_out=ac[:, 0:1]).then_inc(ac_ready, 1)
                    dve.wait_ge(m_ready, now)
                    v.reciprocal(sv[:, before, 0:1], mx)
                    dve.wait_ge(ac_ready, now)
                    v.transpose(tr, ac.unsqueeze(2).broadcast_to([P, 2, 32])).then_inc(T_ready, 1)
                    dve.wait_ge(s_ready, now)
                    v.scalar_tensor_tensor(hr[:, slot, :], vv, sv[:, before, 1:2], ur[:, slot, :], ALU.mult, ALU.add)\
                        .then_inc(h_ready, 1)
                    dve.wait_ge(T_ready, now)
                    v.tensor_tensor_reduce(out=junkq.rearrange("p (w c) -> p w c", w=2), in0=tr2, in1=svb(before),
                                           scale=1.0 / CLAMP ** 2, scalar=ring_be[:, slot, 1:2],
                                           op0=ALU.mult, op1=ALU.add, accum_out=qv).then_inc(q_ready, 1)
            dve.wait_ge(q_ready, NT + 1 + BLK)
            v.tensor_scalar(mx, qv, 1.0, None, ALU.max).then_inc(m_ready, 1)

            def last_product(i):
                f = i % 2
                dve.wait_ge(silu_done, i + 1)
                v.tensor_tensor(sl[:, f], sl[:, f], yl[:, i], ALU.mult).then_inc(f_mul, 1)

            for i in range(CH):
                f = i % 2
                dve.wait_ge(g_half, i + 1)
                if i >= 2:
                    dve.wait_ge(silu_done, i - 1)
                for b in range(NB):
                    last = v.scalar_tensor_tensor(fm[:, f, b, :], g1[i][:, b, :], wsel[:, 1, b * CH + i:b * CH + i + 1],
                                                  g0[:, i, b, :], ALU.mult, ALU.add)
                last.then_inc(f_ready, 1)
                if i >= 1:
                    last_product(i - 1)
            last_product(CH - 1)

        @block.scalar
        def _(act):
            a = nc.scalar
            links = [0]

            def link(ins):
                links[0] += 1
                ins.then_inc(act_chain, 1)
                act.wait_ge(act_chain, links[0])

            act.dma_start(dpb, dpar.rearrange("(a d) -> a d", a=1).broadcast_to([P, D])).then_inc(ld_d, 16)
            act.dma_start(wb_sb, wb.rearrange("(k p) m -> p k m", p=P)).then_inc(ld_w, 16)
            act.dma_start(wc_sb, wc.rearrange("(k p) m -> p k m", p=P)).then_inc(ld_w, 16)
            act.dma_start(wg_sb, w_g.rearrange("(k p) m -> p k m", p=P)).then_inc(ld_w, 16)
            act.dma_start(alog.rearrange("p (k n) -> p k n", k=DH), a_log.rearrange("(k p) n -> p k n", p=P)).then_inc(ld_v, 16)
            act.dma_start(bdt_sb, bdt.rearrange("(k p) -> p k", p=P), allow_slow_non_contiguous=True).then_inc(ld_v, 16)
            act.wait_ge(ld_v, 32)
            act.wait_ge(consts, CONSTS)
            a.activation(alog, alog, ACT.Tanh, scale=0.1).then_inc(a_tanh, 1)
            act.wait_ge(a_tanh, 1)
            a.activation(alog, alog, ACT.Exp, scale=10.0).then_inc(a_exp, 1)
            a.preload_act_table_set("natural_log_exp_and_others")
            def turned(i):
                act.wait_ge(xt_ps, i + 1)
                for k in range(DH):
                    last = a.activation(xnT[:, i, k].rearrange("p b t -> p (b t)"), ps[k][:, :], ACT.Copy)
                last.then_inc(xt_sb, 1)

            turned(0)
            for i in range(CH):
                if i + 1 < CH:
                    turned(i + 1)
                act.wait_ge(z_ps, i + 1)
                if i >= 2:
                    act.wait_ge(sp_ready, i - 1)
                for k in range(DH):
                    a.activation(rel[:, i % 2, k, :], ps[Z_BANKS[i % 2][k]][:, :], ACT.Relu, bias=bdt_sb[:, k:k + 1])
                    last = a.activation(spl[:, i, k, :], ps[Z_BANKS[i % 2][k]][:, :], ACT.Abs, bias=bdt_sb[:, k:k + 1])
                last.then_inc(z_used, 1)
                act.wait_ge(z_used, i + 1)
                link(a.activation(spl[:, i], spl[:, i], ACT.Exp, scale=-1.0))
                a.activation(spl[:, i], spl[:, i], ACT.Ln, bias=1.0).then_inc(sp_half, 1)

            def soft_clamp(i):
                act.wait_ge(sp_ready, i + 1)
                a.activation(spl[:, i], spl[:, i], ACT.Tanh, bias=dtbias[:, :], scale=SHARP / (DT_R + 1e-8)).then_inc(th_ready, 1)

            def tanh_ops(f, first, count, dt_=None):
                src = (stage[:, f, 0, :] if dt_ is None else dt_).rearrange("p (k b t) -> p b k t", b=NB, k=DH)
                dst = tanhb[:, f, :, :].rearrange("p (b k n) t -> p b k n t", b=NB, k=DH)
                for c in range(first, first + count):
                    k, n_ = divmod(c, NS)
                    last = a.activation(dst[:, :, k, n_, :], src[:, :, k, :], ACT.Tanh, scale=a16[:, c:c + 1])
                return last

            def decay_ops(f):
                for c in range(4):
                    flat = tanhb[:, f, c * 32:(c + 1) * 32, :].rearrange("p s t -> p (s t)")
                    last = a.activation(flat, flat, ACT.Exp, scale=16.0)
                return last

            for i in range(CH):
                act.wait_ge(bc_ps, i + 1)
                a.activation(be[:, i * P:(i + 1) * P, 0], ps[BC_BANKS[i % 2]][:, 0:P], ACT.Copy)
                a.activation(ccol[:, BLK + i * P:BLK + (i + 1) * P], ps[BC_BANKS[i % 2]][:, P:2 * P], ACT.Copy).then_inc(bc_sb, 1)
                if i < 3:
                    soft_clamp(i)
                elif i == 3:
                    act.wait_ge(gap_ready, 1)
                    a.activation(pw[:, 3, :], pw[:, 0, :], ACT.Exp).then_inc(gap_exp, 1)
            for i in range(CH):
                if i + 3 < CH:
                    soft_clamp(i + 3)
                act.wait_ge(fst_ready, i + 1)
                if i == 0:
                    act.wait_ge(sp_ready, CH)
                if i >= 1:
                    act.wait_ge(e_ps, i)
                a.activation(sq.rearrange("p k (b t) -> p k b t", b=NB), dxc[:, i % 2].rearrange("p (t b k) -> p k b t", b=NB, k=DH),
                             ACT.Square).then_inc(sq_ready, 1)
                if i == 0:
                    act.wait_ge(xn_out, 16 * CH)
                    act.wait_ge(dxn_ready, CH)
                    act.wait_ge(a_ready, 1)
                    act.wait_ge(dt0_ready, 1)
                last = tanh_ops(0, 4 * i, 4, dt0)
            last.then_inc(tanh_done, 1)
            act.wait_ge(sq_ready, CH)
            act.wait_ge(tanh_done, 1)
            decay_ops(0).then_inc(decay_ready, 1)
            act.sem_inc(loop_go, 1)
            act.wait_ge(loop_go, 5)
            act.sem_inc(da_done, 2)
            act.sem_inc(u_done, 1)
            act.sem_inc(gelu_done, 2)
            act.sem_inc(ye_sb, 1)
            act.sem_inc(yrow_free, 1)


            def inputs_out_of_psum(n):
                act.wait_ge(x_ps, n + 1)
                a.activation(xin, ps[3][:, P:2 * P], ACT.Copy).then_inc(x_sb, 1)

            inputs_out_of_psum(0)
            def y_out_of_psum(n):
                act.wait_ge(y_done, n + 2)
                act.wait_ge(y_out, n * 16 + 1)
                a.activation(ysb, ps[3][:, 0:P], ACT.Copy).then_inc(y_sb, 1)

            with act.Fori(0, CH) as m:
                for g in range(BPB):
                    half, f = g % 2, g // 4
                    act.wait_ge(q_ready, m * P + (g * BLK + 1))
                    a.activation(ring_be[:, half * BLK:(half + 1) * BLK, :], be[:, bass.ds(m * P + g * BLK, BLK), :],
                                 ACT.Copy).then_inc(be_stage, 1)
                    for q in range(QPB):
                        t = half * BLK + q * QUAD
                        quads = m * (P // QUAD) + (g * QPB + q)
                        if q == 1:
                            y_out_of_psum(m * BPB + g)
                        act.wait_ge(ta_ps, quads + 2)
                        a.activation(da[:, t:t + QUAD, :].rearrange("p t d -> p (t d)"), ps[q % 2][:, :], ACT.Copy)\
                            .then_inc(da_done, 1)
                        if q == 0:
                            act.wait_ge(be_stage, m * BPB + (g + 1))
                        act.wait_ge(tu_ps, quads + 1)
                        for j in range(QUAD):
                            last = a.activation(ur[:, t + j, :], ps[2][:, j * P:(j + 1) * P], ACT.Copy,
                                                scale=ring_be[:, t + j, 0:1])
                        last.then_inc(u_done, 1)
                        for kind, i, j, _ in by_quad[g * QPB + q]:
                            if kind == "up":
                                if j == 0:
                                    act.wait_ge(mm2_ps, m * (TPE * 2) + (i * 2 + 1))
                                act.wait_ge(mm1_ps, m * (TPE * FC // 2) + (i * FC // 2 + j + 2))
                                a.activation(hid[:, 2 * j:2 * j + 2, :].rearrange("p c s -> p (c s)"), ps[4 + j % 2][:, :],
                                             ACT.Gelu).then_inc(gelu_done, 1)
                            elif kind == "turn":
                                act.wait_ge(xt_tp, m * TPE + (i + 1))
                                a.activation(xt.rearrange("p k s -> p (k s)"), ps[6][:, :], ACT.Copy).then_inc(xt_in, 1)
                            elif j == 1:
                                act.wait_ge(mm2_ps, m * (TPE * 2) + (i * 2 + 3))
                                act.wait_ge(yrow_free, m * TPE + (i + 1))
                                a.activation(yrow.rearrange("p c d -> p (c d)"), ps[7][:, :], ACT.Copy).then_inc(ye_sb, 1)
                        if q == QPB - 1:
                            inputs_out_of_psum(m * BPB + (g + 1))
                        if g % 4 == 0 and q == 0:
                            act.wait_ge(stage_in, m * 64 + (32 * (f + 2)))
                            act.wait_ge(ta_ps, m * (P // QUAD) + (f * (HALF // QUAD) + 1))
                        last = tanh_ops(1 - f, 2 * (QPB * (g % 4) + q), 2)
                    if g % 4 == 3:
                        last.then_inc(tanh_done, 1)
                        act.wait_ge(tanh_done, m * 2 + (f + 2))
                        decay_ops(1 - f).then_inc(decay_ready, 1)
            act.sem_inc(u_done, 1)
            for n in range(NBLK, NBLK + 2):
                y_out_of_psum(n)
            def first_choice(i):
                act.wait_ge(fin[i], 64)
                for b in range(NB):
                    last = a.activation(g0[:, i, b, :], g0[:, i, b, :], ACT.Copy, scale=wsel[:, 0, b * CH + i:b * CH + i + 1])
                last.then_inc(g_half, 1)

            first_choice(0)
            for i in range(CH):
                if i + 1 < CH:
                    first_choice(i + 1)
                act.wait_ge(f_ready, i + 1)
                if i >= 2:
                    act.wait_ge(o_ready, i - 1)
                a.activation(sl[:, i % 2], fm[:, i % 2], ACT.Silu).then_inc(silu_done, 1)

        @block.tensor
        def _(pe):
            t = nc.tensor
            pe.wait_ge(consts, CONSTS)
            pe.wait_ge(ld_w, 64)
            def turn(i):
                pe.wait_ge(xn_ready, i + 1)
                if i >= 1:
                    pe.wait_ge(xt_sb, i)
                for k in range(DH):
                    for b in range(NB):
                        last = t.transpose(ps[k][:, b * P:(b + 1) * P], xnat[:, b, i, k * P:(k + 1) * P], ident[:, :])
                last.then_inc(xt_ps, 1)

            turn(0)
            for i in range(CH):
                pe.wait_ge(xt_sb, i + 1)
                if i + 1 < CH:
                    turn(i + 1)
                if i >= 2:
                    pe.wait_ge(z_used, i - 1)
                for h in range(DH):
                    for k in range(DH):
                        last = t.matmul(ps[Z_BANKS[i % 2][h]][:, :], wdt_sb[:, k, h * P:(h + 1) * P],
                                        xnT[:, i, k].rearrange("p b t -> p (b t)"), start=k == 0, stop=k == DH - 1)
                last.then_inc(z_ps, 1)
                for b in range(NB):
                    j = b * CH + i
                    for k in range(DH):
                        last = t.matmul(ps[6][:, j * NE:(j + 1) * NE], xnT[:, i, k, b, :], wg_sb[:, k, :],
                                        start=k == 0, stop=k == DH - 1)
                if i == CH - 1:
                    last.then_inc(lg_ps, 1)

            def b_and_c(i):
                if i >= 2:
                    pe.wait_ge(bc_sb, i - 1)
                for w, sbw in enumerate((wb_sb, wc_sb)):
                    for b in range(NB):
                        for k in range(DH):
                            last = t.matmul(ps[BC_BANKS[i % 2]][32 * b:32 * b + 32, w * P:(w + 1) * P], sbw[:, k, :], xnT[:, i, k, b, :],
                                            start=k == 0, stop=k == DH - 1)
                last.then_inc(bc_ps, 1)

            for i in range(CH // 2):
                b_and_c(i)
            pe.wait_ge(rt_in, 1)
            pe.wait_ge(z_used, CH)
            flat = ohb.rearrange("p e k j -> p (e k j)")
            t.matmul(ps[7][:, :], lows, flat, start=True, stop=True)
            t.matmul(ps[6][:, :], ones[:, :], flat, start=True, stop=True).then_inc(rank_ps, 1)
            for i in range(CH // 2, CH):
                b_and_c(i)

            def slots(n):
                pe.wait_ge(lo_ready, n + 1)
                pe.wait_ge(hi_ready, n + 1)
                for c in range(8):
                    last = t.matmul(ps[7][:, 0:SC], lohot[:, n % 2, c, :], hirow[:, n % 2, c, :],
                                    start=n == 0 and c == 0, stop=n == CH - 1 and c == 7)
                last.then_inc(hot_used, 1)

            for i in range(CH):
                pe.wait_ge(sq_ready, i + 1)
                if i >= 1:
                    pe.wait_ge(e_used, i)
                for b in range(NB):
                    for k in range(DH):
                        t.matmul(ps[5][32 * b:32 * b + 32, 0:P], ones[:, 0:32], sq[:, k, b * P:(b + 1) * P],
                                 start=k == 0, stop=k == DH - 1)
                pe.wait_ge(sqb_ready, i + 1)
                t.matmul(ps[5][:, P:2 * P], bsum[:, :], sqb, start=True, stop=True).then_inc(e_ps, 1)
                if i >= 1:
                    slots(i - 1)
            pe.wait_ge(e_ps, CH)
            pe.wait_ge(route_ready, 1)
            pe.sem_inc(loop_go, 1)
            slots(CH - 1)
            pe.wait_ge(loop_go, 5)
            pe.sem_inc(mm1_ps, 1)
            pe.sem_inc(mm2_ps, 1)
            pe.sem_inc(y_done, 1)
            pe.sem_inc(ta_ps, 1)

            def turn_rows():
                for k in range(DH):
                    for c in range(2):
                        last = t.transpose(ps[6][:, k * TS + c * P:k * TS + (c + 1) * P], xrow[:, c, k * P:(k + 1) * P], ident[:, :])
                return last

            def turn_inputs(f, block_):
                c = block_ * P
                return t.transpose(ps[3][:, P:2 * P], stage[:, f, 1, c:c + P], ident[:, :])

            pe.wait_ge(stage_in, 32)
            turn_inputs(0, 0).then_inc(x_ps, 1)

            def output(n, count, half):
                pe.wait_ge(win_ready, n + 1)
                pe.wait_ge(h_ready, count)
                pe.wait_ge(dx_in, (n + 1) * 16)
                t.matmul(ps[3][:, 0:P], ident[:, :], dxt, start=True, stop=False)
                for j in range(BLK):
                    last = t.matmul(ps[3][:, 0:P], win[:, j, BLK - 1 - j:2 * BLK - 1 - j, :].rearrange("p c g -> p (c g)"), hr[:, half * BLK + j, :],
                                    start=False, stop=j == BLK - 1)
                last.then_inc(y_done, 1)

            pe.wait_ge(h_ready, BLK + 1)
            with pe.Fori(0, CH) as m:
                for g in range(BPB):
                    f = g // 4
                    if g % 4 == 0:
                        pe.wait_ge(decay_ready, m * 2 + (f + 1))
                    pe.wait_ge(x_sb, m * BPB + (g + 1))
                    for q in range(QPB):
                        quads = m * (P // QUAD) + (g * QPB + q)
                        if q == 1:
                            output(m * BPB + g, m * P + (g * BLK + 1), g % 2)
                        pe.wait_ge(da_done, quads + 1)
                        for j in range(QUAD):
                            s = (g % 4) * BLK + q * QUAD + j
                            last = t.transpose(ps[q % 2][:, j * P:(j + 1) * P], tanhb[:, f, :, s], ident[:, :])
                        last.then_inc(ta_ps, 1)
                        pe.wait_ge(u_done, quads + 1)
                        for j in range(QUAD):
                            last = t.matmul(ps[2][:, j * P:(j + 1) * P], pick[:, q * QUAD + j, :], xin, start=True, stop=True)
                        last.then_inc(tu_ps, 1)
                        for kind, i, j, _ in by_quad[g * QPB + q]:
                            if kind == "up":
                                if j == 0:
                                    if i == 0:
                                        pe.wait_ge(wf_in, m * 16 + 16)
                                    pe.wait_ge(xt_in, m * TPE + (i + 1))
                                pe.wait_ge(gelu_done, m * (TPE * FC // 2) + (i * FC // 2 + j + 1))
                                for c in range(2):
                                    for k in range(DH):
                                        last = t.matmul(ps[4 + j % 2][:, c * TS:(c + 1) * TS],
                                                        wf[:, k, (2 * j + c) * P:(2 * j + c + 1) * P], xt[:, k, :],
                                                        start=k == 0, stop=k == DH - 1)
                                last.then_inc(mm1_ps, 1)
                            elif kind == "turn":
                                pe.wait_ge(xrow_in, m * (32 * TPE) + 32 * (i + 1))
                                turn_rows().then_inc(xt_tp, 1)
                            else:
                                if j == 0:
                                    if i == 0:
                                        pe.wait_ge(wp_in, m * 16 + 16)
                                    pe.wait_ge(gelu_done, m * (TPE * FC // 2) + ((i + 1) * FC // 2 + 2))
                                    pe.wait_ge(ye_sb, m * TPE + (i + 1))
                                for k in range(FC):
                                    last = t.matmul(ps[7][:, j * D:(j + 1) * D], hid[:, k, j * P:(j + 1) * P], wp[:, k, :],
                                                    start=k == 0, stop=k == FC - 1)
                                last.then_inc(mm2_ps, 1)
                    pe.wait_ge(y_sb, m * BPB + (g + 1))
                    if g % 4 == 3:
                        pe.wait_ge(stage_in, m * 64 + 32 * (f + 2))
                    turn_inputs((g + 1) // 4 % 2, (g + 1) % 4).then_inc(x_ps, 1)
            pe.wait_ge(x_sb, NBLK + 1)
            for n in range(NBLK, NBLK + 2):
                if n > NBLK:
                    pe.wait_ge(y_sb, n)
                output(n, (n - 1) * BLK + BLK + 1, n % 2)


def kernel(**inputs):
    import numpy as _np
    import concourse.bacc as _bacc
    from concourse import mybir as _mybir
    from concourse.bass_utils import run_bass_kernel_spmd as _run

    def state_columns(w):
        wt = _np.transpose(w)
        return _np.ascontiguousarray(_np.concatenate([wt] * DH, axis=1))

    laid = {
        "x": inputs["L0_attn_x"],
        "wdtT": _np.ascontiguousarray(_np.transpose(inputs["L0_attn_Wdt"])),
        "bdt": inputs["L0_attn_bdt"],
        "wb": state_columns(inputs["L0_attn_WB"]),
        "wc": state_columns(inputs["L0_attn_WC"]),
        "a_log": inputs["L0_attn_A_log"],
        "dpar": inputs["L0_attn_Dp"],
        "w_g": inputs["L0_ffn_w_g"],
        "c_fc": inputs["L0_ffn_c_fc"],
        "c_proj": inputs["L0_ffn_c_proj"],
    }
    nc = _bacc.Bacc("TRN2", target_bir_lowering=False, num_devices=1)
    arrays, args = {}, []
    for name, a in laid.items():
        a = _np.ascontiguousarray(a)
        arrays[f"in_{name}"] = a
        args.append(nc.dram_tensor(f"in_{name}", a.shape, _mybir.dt.from_np(a.dtype), kind="ExternalInput").ap())
    out = nc.dram_tensor("out_0", (NB, NT, D), _mybir.dt.float32, kind="ExternalOutput").ap()
    build(nc, *args, out)
    r = _run(nc, [arrays], core_ids=[0])
    return r.results[0]["out_0"]
```
